# Optimizing a Trainium2 kernel written in Bass

```python
import numpy as np
import jax
import jax.numpy as jnp

def _softmax(x, axis=-1):
    return jax.nn.softmax(x, axis=axis)

def _gelu(x):
    return jax.nn.gelu(x, approximate=True)

def _silu(x):
    return jax.nn.silu(x)

def _sigmoid(x):
    return jax.nn.sigmoid(x)

def _layernorm(x, axis=-1, eps=1e-05):
    m = jnp.mean(x, axis=axis, keepdims=True)
    v = jnp.var(x, axis=axis, keepdims=True)
    return (x - m) / jnp.sqrt(v + eps)

def _scatter_add(tgt, idx, src, axis=0):
    return tgt.at[idx].add(src)

def _segment_sum(src, seg, n):
    return jax.ops.segment_sum(src, seg, n)
kernel_name = 'mk_adaln_d1_jaxref_r8_c0fe92'

def setup_inputs(seed: int=0):
    np.random.seed(seed)
    _w = jnp.asarray

    def _L0_attn_setup():
        import jax, jax.numpy as jnp
        import numpy as np
        H = 512
        D = 1024
        N = 16
        K = 4
        R = 32
        BATCH = 1
        L = 256
        EPS = 1e-06

        def _rmsnorm(x, w):
            return x * jax.lax.rsqrt(jnp.mean(x * x, axis=-1, keepdims=True) + EPS) * w
        key = jax.random.key(seed)
        ks = jax.random.split(key, 10)
        s = 0.02
        return {'hidden_states': jax.random.normal(ks[0], (BATCH, L, H), jnp.float32), 'W_in': jax.random.normal(ks[1], (2 * D, H), jnp.float32) * s, 'conv_w': jax.random.normal(ks[2], (D, K), jnp.float32) * s, 'conv_b': jax.random.normal(ks[3], (D,), jnp.float32) * s, 'Wx': jax.random.normal(ks[4], (R + 2 * N, D), jnp.float32) * s, 'dt_ln_w': jnp.ones((R,), jnp.float32), 'b_ln_w': jnp.ones((N,), jnp.float32), 'c_ln_w': jnp.ones((N,), jnp.float32), 'Wdt': jax.random.normal(ks[5], (D, R), jnp.float32) * s, 'dt_bias': jax.random.normal(ks[6], (D,), jnp.float32) * s, 'A': -jnp.exp(jax.random.normal(ks[7], (D, N), jnp.float32) * 0.5), 'D_param': jnp.ones((D,), jnp.float32), 'W_out': jax.random.normal(ks[8], (H, D), jnp.float32) * s}
    _L0_attn_in = _L0_attn_setup()

    def _L0_ffn_setup():
        import jax, jax.numpy as jnp
        import numpy as np
        NUM_EXPERTS = 8
        RANK = 32
        ALPHA = 16.0
        TOP_K = 2
        TEMPERATURE = 1.0
        GAMMA = 0.5
        SOFT_TOPK_TEMP = 0.5
        N_GRAM = 2
        EPS = 1e-06
        key = jax.random.key(seed)
        ks = jax.random.split(key, 6)
        d_in, d_out = (512, 512)
        Bsz, T = (4, 256)
        x = jax.random.normal(ks[0], (Bsz, T, d_in), dtype=jnp.float32)
        W = jax.random.normal(ks[1], (d_out, d_in), dtype=jnp.float32) / np.sqrt(d_in)
        b = jax.random.normal(ks[2], (d_out,), dtype=jnp.float32) * 0.01
        A = jax.random.normal(ks[3], (d_in, RANK), dtype=jnp.float32) / np.sqrt(d_in)
        Bmat = jax.random.normal(ks[4], (RANK, d_out), dtype=jnp.float32) * 0.01
        LiMEs = jax.random.normal(ks[5], (NUM_EXPERTS, RANK), dtype=jnp.float32) * 0.1
        return {'x': x, 'W': W, 'b': b, 'A': A, 'Bmat': Bmat, 'LiMEs': LiMEs}
    _L0_ffn_in = _L0_ffn_setup()
    _L0_c = _w((lambda *s: np.random.randn(*s).astype(np.float32) * 0.05)(1, 512))
    _L0_wmod = _w((lambda *s: np.random.randn(*s).astype(np.float32) * 0.05)(512, 6 * 512) * 512 ** (-0.5))
    _d = {'L0_attn_hidden_states': _L0_attn_in['hidden_states'], 'L0_attn_W_in': _L0_attn_in['W_in'], 'L0_attn_conv_w': _L0_attn_in['conv_w'], 'L0_attn_conv_b': _L0_attn_in['conv_b'], 'L0_attn_Wx': _L0_attn_in['Wx'], 'L0_attn_dt_ln_w': _L0_attn_in['dt_ln_w'], 'L0_attn_b_ln_w': _L0_attn_in['b_ln_w'], 'L0_attn_c_ln_w': _L0_attn_in['c_ln_w'], 'L0_attn_Wdt': _L0_attn_in['Wdt'], 'L0_attn_dt_bias': _L0_attn_in['dt_bias'], 'L0_attn_A': _L0_attn_in['A'], 'L0_attn_D_param': _L0_attn_in['D_param'], 'L0_attn_W_out': _L0_attn_in['W_out'], 'L0_ffn_W': _L0_ffn_in['W'], 'L0_ffn_b': _L0_ffn_in['b'], 'L0_ffn_A': _L0_ffn_in['A'], 'L0_ffn_Bmat': _L0_ffn_in['Bmat'], 'L0_ffn_LiMEs': _L0_ffn_in['LiMEs'], 'L0_c': _L0_c, 'L0_wmod': _L0_wmod}
    _x0 = _d['L0_attn_hidden_states']
    _d['L0_attn_hidden_states'] = jax.random.normal(jax.random.fold_in(jax.random.key(seed), 1), (1, 2048, 512), dtype=_x0.dtype)
    del _x0
    return _d

def reference(L0_attn_hidden_states, L0_attn_W_in, L0_attn_conv_w, L0_attn_conv_b, L0_attn_Wx, L0_attn_dt_ln_w, L0_attn_b_ln_w, L0_attn_c_ln_w, L0_attn_Wdt, L0_attn_dt_bias, L0_attn_A, L0_attn_D_param, L0_attn_W_out, L0_ffn_W, L0_ffn_b, L0_ffn_A, L0_ffn_Bmat, L0_ffn_LiMEs, L0_c, L0_wmod):

    def _L0_attn_ref(hidden_states, W_in, conv_w, conv_b, Wx, dt_ln_w, b_ln_w, c_ln_w, Wdt, dt_bias, A, D_param, W_out):
        import jax, jax.numpy as jnp
        import numpy as np
        H = 512
        D = 1024
        N = 16
        K = 4
        R = 32
        BATCH = 1
        L = 256
        EPS = 1e-06

        def _rmsnorm(x, w):
            return x * jax.lax.rsqrt(jnp.mean(x * x, axis=-1, keepdims=True) + EPS) * w
        proj = hidden_states @ W_in.T
        u, gate = jnp.split(proj, 2, axis=-1)
        x = jnp.transpose(u, (0, 2, 1))
        x = jax.lax.conv_general_dilated(x, conv_w[:, None, :], window_strides=(1,), padding=[(K - 1, 0)], dimension_numbers=('NCH', 'OIH', 'NCH'), feature_group_count=D)
        u = jax.nn.silu(jnp.transpose(x, (0, 2, 1)) + conv_b)
        ssm_p = u @ Wx.T
        dt, Bm, Cm = jnp.split(ssm_p, [R, R + N], axis=-1)
        dt = _rmsnorm(dt, dt_ln_w)
        Bm = _rmsnorm(Bm, b_ln_w)
        Cm = _rmsnorm(Cm, c_ln_w)
        delta = jax.nn.softplus(dt @ Wdt.T + dt_bias)

        def step(state, xs):
            d_t, B_t, C_t, u_t = xs
            dA = jnp.exp(d_t[..., None] * A)
            state = dA * state + (d_t * u_t)[..., None] * B_t[:, None, :]
            y_t = jnp.einsum('bdn,bn->bd', state, C_t)
            return (state, y_t)
        init = jnp.zeros((hidden_states.shape[0], D, N), hidden_states.dtype)
        xs = (jnp.swapaxes(delta, 0, 1), jnp.swapaxes(Bm, 0, 1), jnp.swapaxes(Cm, 0, 1), jnp.swapaxes(u, 0, 1))
        _, ys = jax.lax.scan(step, init, xs)
        y = jnp.swapaxes(ys, 0, 1) + u * D_param
        y = y * jax.nn.silu(gate)
        return y @ W_out.T

    def _L0_ffn_ref(x, W, b, A, Bmat, LiMEs):
        import jax, jax.numpy as jnp
        import numpy as np
        NUM_EXPERTS = 8
        RANK = 32
        ALPHA = 16.0
        TOP_K = 2
        TEMPERATURE = 1.0
        GAMMA = 0.5
        SOFT_TOPK_TEMP = 0.5
        N_GRAM = 2
        EPS = 1e-06
        Bsz, T, d_in = x.shape
        E = LiMEs.shape[0]
        scaling = ALPHA / RANK
        H = jnp.einsum('btd,od->bto', x, W) + b
        z = jnp.einsum('btd,dr->btr', x, A)
        anchors = jnp.arange(N_GRAM - 1, T, N_GRAM)
        H_slice = H[:, anchors, :E]
        delta_slice = jnp.einsum('bar,er->bae', z[:, anchors], LiMEs)
        H_scale = jnp.maximum(jnp.max(jnp.abs(H_slice)), EPS)
        d_scale = jnp.maximum(jnp.max(jnp.abs(delta_slice)), EPS)
        logits = ((1.0 - GAMMA) * (H_slice / H_scale) + GAMMA * (delta_slice / d_scale)) / TEMPERATURE
        probs = jax.nn.softmax(logits, axis=-1)
        topk_vals, _ = jax.lax.top_k(probs, TOP_K)
        thresh = topk_vals[..., -1:]
        mask = jax.nn.sigmoid((probs - thresh) / SOFT_TOPK_TEMP)
        weights = probs * mask
        weights = weights / (jnp.sum(weights, axis=-1, keepdims=True) + 1e-09)
        weights_full = jnp.repeat(weights, N_GRAM, axis=1)
        p_mix = jnp.einsum('bte,er->btr', weights_full, LiMEs)
        delta = jnp.einsum('btr,ro->bto', z * p_mix, Bmat) * scaling
        return H + delta
    x = L0_attn_hidden_states
    mod = (_silu(L0_c) @ L0_wmod).reshape(L0_c.shape[0], 6, 1, -1)
    sa, ca, ga, sb, cb, gb = (mod[:, 0], mod[:, 1], mod[:, 2], mod[:, 3], mod[:, 4], mod[:, 5])
    ga = (2 * (ga >= 0) - 1) * jnp.maximum(jnp.abs(ga), 0.25)
    gb = (2 * (gb >= 0) - 1) * jnp.maximum(jnp.abs(gb), 0.25)
    h = _layernorm(x, axis=-1) * (1 + ca) + sa
    x = x + ga * _L0_attn_ref(h, L0_attn_W_in, L0_attn_conv_w, L0_attn_conv_b, L0_attn_Wx, L0_attn_dt_ln_w, L0_attn_b_ln_w, L0_attn_c_ln_w, L0_attn_Wdt, L0_attn_dt_bias, L0_attn_A, L0_attn_D_param, L0_attn_W_out)
    h = _layernorm(x, axis=-1) * (1 + cb) + sb
    x = x + gb * _L0_ffn_ref(h, L0_ffn_W, L0_ffn_b, L0_ffn_A, L0_ffn_Bmat, L0_ffn_LiMEs)
    return x

_drawn_inputs = setup_inputs


def setup_inputs(seed=0):
    import zlib

    import numpy as np

    out = dict(_drawn_inputs(seed))
    spreads = {'L0_attn_dt_ln_w': (1.0, 0.6),
     'L0_attn_b_ln_w': (1.0, 0.6),
     'L0_attn_c_ln_w': (1.0, 0.6),
     'L0_attn_D_param': (1.0, 0.6)}
    factors = {'L0_attn_W_in': 8.0,
     'L0_attn_conv_w': 8.0,
     'L0_attn_conv_b': 8.0,
     'L0_attn_Wx': 8.0,
     'L0_attn_Wdt': 8.0,
     'L0_attn_dt_bias': 8.0,
     'L0_attn_A': 8.0,
     'L0_attn_W_out': 8.0,
     'L0_ffn_b': 64.0,
     'L0_ffn_A': 64.0,
     'L0_ffn_Bmat': 64.0,
     'L0_ffn_LiMEs': 64.0,
     'L0_ffn_W': 7.171}
    for name, (base, spread) in spreads.items():
        noise = np.random.default_rng([zlib.crc32(name.encode()), seed]).standard_normal(out[name].shape)
        drawn = base * np.exp(spread * noise) if base else spread * noise
        out[name] = jnp.asarray(drawn.astype(out[name].dtype))
    for name, factor in factors.items():
        out[name] = (out[name] * factor).astype(out[name].dtype)
    return out
```

```python
import concourse.bass as bass
from concourse import mybir
from contextlib import ExitStack

L, H, D, NS, R, K = 2048, 512, 1024, 16, 32, 4
E, RANK = 8, 32
P = 128
T = 256
NC = L // T
TT = T // P
DB = D // P
KT = H // P
HB = DB // 2
PAIRS = DB // 2
ITEMS = 2 * NS
BANKS = 2 * ITEMS
USES = 8
GROUP = 2
SLOT_LOADS = NS // GROUP // 2
XP = R + 2 * NS


class Chunk:

    def __init__(self, k, turn, par):
        self.k, self.turn, self.par = k, turn, par
        self.links = {}

    def first(self):
        return isinstance(self.k, int) and self.k == 0

    def later(self, n):
        return not isinstance(self.k, int) or self.k >= n


def static(k):
    return Chunk(k, k // 2, k % 2)


def build(nc, x, w_in, conv_w, conv_b, w_x, dt_w, b_w, c_w, w_dt, dt_bias, a_neg, d_par, w_out,
          ffn_w, ffn_b, ffn_a, bmat, limes, limes_t, cond, wmod, out):
    f32 = mybir.dt.float32
    ALU = mybir.AluOpType
    ACT = mybir.ActivationFunctionType
    AX = mybir.AxisListType.X
    with ExitStack() as ctx:
        def sb(name, *shape):
            return ctx.enter_context(nc.sbuf_tensor(name, list(shape), f32))

        def bank(name):
            return ctx.enter_context(nc.psum_tensor(name, [P, 512], f32))

        def sem(name):
            return ctx.enter_context(nc.semaphore(name))

        win = sb("win", P, KT, 2 * D)
        wx = sb("wx", P, DB, XP)
        wdt = sb("wdt", R, D)
        wout = sb("wout", P, DB, H)
        fw = sb("fw", P, KT, H)
        fw8 = sb("fw8", P, KT, E)
        fa = sb("fa", P, KT, RANK)
        fb = sb("fb", 1, H)
        fb8 = sb("fb8", 1, E)
        bm = sb("bm", RANK, H)
        lim = sb("lim", E, RANK)
        limt = sb("limt", RANK, E)
        an = sb("an", P, NS, DB)
        cw = sb("cw", P, DB, K)
        cb = sb("cb", P, DB)
        dtb = sb("dtb", P, DB)
        dp = sb("dp", P, DB)
        dtw = sb("dtw", R, 1)
        bw = sb("bw", P, NS)
        cwt = sb("cwt", P, NS)
        cnd = sb("cnd", P, KT)
        cnt = sb("cnt", P, 2, KT)
        mcol = sb("mcol", P, 4, KT)
        ident = sb("ident", P, P)
        ones = sb("ones", P, P)
        diag_d = sb("diag_d", P, DB, P)
        odd = sb("odd", P, 1)
        xt = [sb(f"xt{i}", P, TT, H) for i in range(2)]
        ht_in = [sb(f"ht_in{i}", P, KT, T) for i in range(2)]
        upre = sb("upre", P, DB, K - 1 + T)
        ub = sb("ub", P, DB, T)
        se = [sb(f"se{i}", P, 2, T) for i in range(2)]
        unused = sb("unused", P, 1)
        fst = sb("fst", P, TT, 6)
        fmv = sb("fmv", P, TT, 2)
        frs = sb("frs", P, TT, 2)
        ssm = sb("ssm", P, TT, XP)
        ssq = sb("ssq", P, TT, XP)
        ms = sb("ms", P, TT, 3)
        mr = sb("mr", P, TT, 3)
        dtn = sb("dtn", P, TT, R)
        bn = sb("bn", P, TT, NS)
        cn = [sb(f"cn{i}", P, TT, NS) for i in range(2)]
        dt_t = sb("dt_t", R, T)
        b_t = sb("b_t", NS, T)
        delta = [sb(f"delta{i}", P, DB, T) for i in range(2)]
        du = [sb(f"du{i}", P, DB, T) for i in range(2)]
        brow = [sb(f"brow{i}", P, GROUP, T) for i in range(2)]
        drive = [sb(f"drive{i}", P, HB, T) for i in range(2)]
        st = [sb(f"st{i}", P, HB, T) for i in range(2)]
        carry = sb("carry", P, NS, DB)
        acc = [sb(f"acc{i}", P, TT, D) for i in range(2)]
        y = sb("y", P, DB, T)
        xr = sb("xr", P, TT, H)
        x2 = y[:, 0:HB, :].rearrange("p a t -> p (a t)").rearrange("p (a h) -> p a h", a=TT)
        h2t = y[:, HB:DB, :]
        cbc = se[0][:].rearrange("p a t -> p (a t)").rearrange("p (k m) -> p k m", k=KT)
        gbc = xr
        bst = sb("bst", P, TT, 6)
        bmv = sb("bmv", P, TT, 2)
        brs = sb("brs", P, TT, 2)
        zk = sb("zk", RANK, T)
        zall = sb("zall", RANK, L)
        hs = sb("hs", P, L // P, E)
        ds = sb("ds", P, L // P, E)
        lt = L // P
        tw = [st[0][:, 0:1, :].rearrange("p a t -> p (a t)")[:, i * lt * E:(i + 1) * lt * E]
              .rearrange("p (a b) -> p a b", b=E) for i in range(2)]
        tw += [st[0][:, 1:3, :].rearrange("p a t -> p (a t)")[:, i * lt * E:(i + 1) * lt * E]
               .rearrange("p (a b) -> p a b", b=E) for i in range(3)]
        tmx = sb("tmx", P, 2)
        tmr = sb("tmr", P, 2)
        tm = sb("tm", P, 4, lt)

        b_dram = nc.dram_tensor("b_rows", [2, NS, T], f32, kind="Internal").ap()
        base_dram = nc.dram_tensor("base", [L, H], f32, kind="Internal").ap()

        decay = [bank(f"decay{i}") for i in range(2)]
        stt = [bank(f"stt{i}") for i in range(2)]
        fp = [bank(f"fp{i}") for i in range(2)]
        bp = [bank(f"bp{i}") for i in range(2)]

        def nothing(c, n):
            pass

        def two(b):
            return b[:, :].rearrange("p (a t) -> p a t", a=2)

        w_loaded = [sem(f"w_loaded{i}") for i in range(4)]
        mod_loaded = sem("mod_loaded")
        const_made = sem("const_made")
        cond_e = sem("cond_e")
        cond_u = sem("cond_u")
        cond_bc = sem("cond_bc")
        mod_full = sem("mod_full")
        mod_abs = sem("mod_abs")
        mod_made = sem("mod_made")
        folded = sem("folded")
        setup_link = sem("setup_link")
        setup_v = sem("setup_v")
        x_in = [sem(f"x_in{i}") for i in range(2)]
        f_full = [sem(f"f_full{i}") for i in range(2)]
        f_used = [sem(f"f_used{i}") for i in range(2)]
        f_var = sem("f_var")
        f_rstd = sem("f_rstd")
        f_xn = sem("f_xn")
        f_conv = sem("f_conv")
        f_e = sem("f_e")
        f_u = sem("f_u")
        f_ms = sem("f_ms")
        f_mrstd = sem("f_mrstd")
        f_bc = sem("f_bc")
        f_ln = sem("f_ln")
        f_du = sem("f_du")
        f_vlink = sem("f_vlink")
        f_alink = sem("f_alink")
        f_glink = sem("f_glink")
        b_out = sem("b_out")
        brow_in = [sem(f"brow_in{i}") for i in range(2)]
        decay_ready = sem("decay_ready")
        scan_done = sem("scan_done")
        drive_ready = sem("drive_ready")
        carry_saved = sem("carry_saved")
        st_turned = sem("st_turned")
        y_added = sem("y_added")
        r_full = [sem(f"r_full{i}") for i in range(2)]
        r_used = [sem(f"r_used{i}") for i in range(2)]
        g_e = sem("g_e")
        g_vlink = sem("g_vlink")
        g_alink = sem("g_alink")
        xr_in = sem("xr_in")
        r_var = sem("r_var")
        r_rstd = sem("r_rstd")
        r_xn = sem("r_xn")
        r_vlink = sem("r_vlink")
        r_alink = sem("r_alink")
        base_out = sem("base_out")
        t_link = sem("t_link")
        t_act = sem("t_act")
        t_pe = sem("t_pe")
        t_red = sem("t_red")
        base_in = sem("base_in")
        out_done = sem("out_done")

        GATE_USES = PAIRS // 2
        F_VLINKS, F_ALINKS, F_GLINKS = 27, 10, 4
        R_VLINKS, R_ALINKS, G_VLINKS, G_ALINKS = 5, 1, PAIRS, PAIRS

        class Links:

            def __init__(self, eng, s, per):
                self.eng, self.s, self.per = eng, s, per

            def __call__(self, c, ins, wait=True):
                n = c.links[self.s.name] = c.links.get(self.s.name, 0) + 1
                ins.then_inc(self.s, 1)
                if wait:
                    self.eng.wait_ge(self.s, self.per * c.k + n)

            def close(self, c):
                assert c.links[self.s.name] == self.per, (self.s.name, c.links[self.s.name])

        out_ready = sem("out_ready")
        base_tiles = [b[:].rearrange("p a b -> p (a b)").rearrange("p (t h) -> p t h", t=4)
                      for b in (delta[0], delta[1], du[0], du[1])]
        w_all = [16 * 10, 16, 16, 16 * 7]
        TAIL_W, TAIL_WT = 19, 5
        wt_all = [ub[0:E, 2 * q:2 * q + 2, :].rearrange("p a b -> p (a b)") for q in range(4)]

        block = ctx.enter_context(nc.Block())

        def over_chunks(eng, front, scan, back, gates):
            c0 = static(0)
            for n in range(NS):
                front(c0, n)

            def chunk(c, prev, nxt):
                for n in range(NS):
                    scan(c, n, prev)
                    if prev is not None:
                        back(prev, n)
                    if nxt is not None:
                        front(nxt, n)
                    gates(c, n)

            chunk(c0, None, static(1))
            chunk(static(1), static(0), static(2))
            with eng.Fori(0, NC // 2 - 2) as m:
                c = [Chunk(2 * m + 1, m, 1), Chunk(2 * m + 2, m + 1, 0), Chunk(2 * m + 3, m + 1, 1),
                     Chunk(2 * m + 4, m + 2, 0)]
                chunk(c[1], c[0], c[2])
                chunk(c[2], c[1], c[3])
            chunk(static(NC - 2), static(NC - 3), static(NC - 1))
            last = static(NC - 1)
            chunk(last, static(NC - 2), None)
            return last

        @block.sync
        def _(sp):
            def load(dst, src, s):
                sp.dma_start(dst, src).then_inc(s, 16)

            def value(e):
                return e if isinstance(e, int) else sp.snap(e)

            load(cnd[:], cond, mod_loaded)
            mods = wmod.rearrange("(k p) (j n) -> j p k n", p=P, j=6)
            spots = [delta[0], delta[1], du[0], du[1], acc[0], acc[1]]
            for j in (0, 1):
                load(spots[j][:].rearrange("p a b -> p (a b)").rearrange("p (k n) -> p k n", k=KT),
                     mods[j], mod_loaded)
            for i in range(2):
                load(xt[i][:], x[0, i * T:(i + 1) * T, :].rearrange("(t p) h -> p t h", p=P), x_in[i])
            load(bw[:], b_w[None, :].broadcast_to([P, NS]), w_loaded[0])
            load(cwt[:], c_w[None, :].broadcast_to([P, NS]), w_loaded[0])
            for dst, src in ((dtw, dt_w), (an, a_neg), (cw, conv_w), (cb, conv_b), (dtb, dt_bias),
                             (dp, d_par), (wx, w_x), (wdt, w_dt)):
                load(dst[:], src, w_loaded[0])
            load(win[:, :, 0:D], w_in[:, :, 0:D], w_loaded[1])
            for j in (2, 3, 4, 5):
                load(spots[j][:].rearrange("p a b -> p (a b)").rearrange("p (k n) -> p k n", k=KT),
                     mods[j], mod_loaded)
            load(win[:, :, D:2 * D], w_in[:, :, D:2 * D], w_loaded[2])
            for dst, src in ((wout, w_out), (fw, ffn_w), (fa, ffn_a), (fb, ffn_b), (bm, bmat),
                             (lim, limes), (limt, limes_t)):
                load(dst[:], src, w_loaded[3])

            def front(c, n):
                if n == 0 and c.later(2):
                    at, done = value(c.k * T), value(USES * (c.k - 2) + 1)
                    sp.wait_ge(f_full[0], done)
                    sp.wait_ge(f_full[1], done)
                    load(xt[c.par][:], x[0, bass.ds(at, T), :].rearrange("(t p) h -> p t h", p=P),
                         x_in[c.par])
                if n == 13:
                    sp.wait_ge(f_used[1], USES * c.k + 6)
                    load(b_dram[c.par], b_t[:], b_out)

            def scan(c, n, prev):
                if n == 0:
                    rows(c, 0)
                    rows(c, 1)
                if n and n % GROUP == 0 and n + GROUP < NS:
                    rows(c, n // GROUP + 1)

            def rows(c, g):
                if g == 0:
                    sp.wait_ge(b_out, 16 * c.k + 16)
                if g >= 2 or c.later(1):
                    sp.wait_ge(drive_ready, ITEMS * c.k + 2 * GROUP * (g - 1))
                load(brow[g % 2][:], b_dram[c.par, GROUP * g:GROUP * (g + 1), :][None].broadcast_to([P, GROUP, T]),
                     brow_in[g % 2])

            def back(c, n):
                if n == 0:
                    at = value(c.k * T)
                    if c.later(1):
                        sp.wait_ge(base_out, 16 * c.k)
                    else:
                        sp.wait_ge(folded, 3)
                    load(xr[:], x[0, bass.ds(at, T), :].rearrange("(t p) h -> p t h", p=P), xr_in)
                if n == 10:
                    at, done = value(c.k * T), value(USES * c.k + GATE_USES + 5)
                    for s in r_used:
                        sp.wait_ge(s, done)
                    load(base_dram[bass.ds(at, T), :].rearrange("(t p) h -> p t h", p=P), xr[:], base_out)

            last = over_chunks(sp, front, scan, back, nothing)
            for n in range(NS):
                back(last, n)
            sp.wait_ge(base_out, 16 * NC)
            sp.wait_ge(y_added, BANKS * NC)
            for q, b in enumerate(base_tiles):
                load(b, base_dram[q * 512:(q + 1) * 512, :].rearrange("(t p) h -> p t h", p=P), base_in)
            for q, b in enumerate(base_tiles):
                sp.wait_ge(out_ready, 4 * (q + 1))
                load(out[0, q * 512:(q + 1) * 512, :].rearrange("(t p) h -> p t h", p=P), b, out_done)
            sp.wait_ge(out_done, 16 * len(base_tiles))


        @block.tensor
        def _(pe):
            def mm(o, a, b, start=True, stop=True):
                return nc.tensor.matmul(o, a, b, start=start, stop=stop)

            pe.wait_ge(cond_u, 1)
            pe.wait_ge(mod_loaded, 16 * 7)
            spots = [delta[0], delta[1], du[0], du[1], acc[0], acc[1]]
            wm = [s[:].rearrange("p a b -> p (a b)").rearrange("p (k n) -> p k n", k=KT) for s in spots]
            for g, j in enumerate((0, 1, 3, 4)):
                for m in range(KT):
                    for q in range(KT):
                        last = mm(bp[0][:, g * KT + m:g * KT + m + 1], wm[j][:, q, m * P:(m + 1) * P],
                                  cnt[:, 1, q:q + 1], q == 0, q == KT - 1)
            last.then_inc(mod_full, 1)
            pe.wait_ge(cond_bc, 1)
            for g, j in enumerate((2, 5)):
                for q in range(KT):
                    last = mm(fp[g][:, :], cbc[:, q, :], wm[j][:, q, :], q == 0, q == KT - 1)
            last.then_inc(mod_full, 1)
            pe.wait_ge(mod_made, 3)
            pe.wait_ge(const_made, 3)

            def free(c, b, u):
                if u or c.later(1):
                    pe.wait_ge(f_used[b], USES * c.k + u)

            def rfree(c, b, u):
                if u or c.later(1):
                    pe.wait_ge(r_used[b], USES * c.k + u)

            def front(c, n):
                if n == 1:
                    pe.wait_ge(f_xn, c.k + 1)
                    for b in range(2):
                        free(c, b, 0)
                        for j in range(2):
                            for tt in range(TT):
                                last = nc.tensor.transpose(
                                    two(fp[b])[:, j, tt * P:(tt + 1) * P],
                                    xt[c.par][:, tt, (2 * b + j) * P:(2 * b + j + 1) * P], ident[:])
                        last.then_inc(f_full[b], 1)
                if 2 <= n < 2 + PAIRS:
                    i = n - 2
                    if i == 0:
                        pe.wait_ge(f_used[0], USES * c.k + 1)
                        pe.wait_ge(f_used[1], USES * c.k + 1)
                        if c.first():
                            pe.wait_ge(w_loaded[1], 16)
                    free(c, i % 2, 1 + i // 2)
                    for j in range(2):
                        for q in range(KT):
                            last = mm(two(fp[i % 2])[:, j, :], win[:, q, (2 * i + j) * P:(2 * i + j + 1) * P],
                                      ht_in[c.par][:, q, :], q == 0, q == KT - 1)
                    last.then_inc(f_full[i % 2], 1)
                if n in (8, 10):
                    h = (n - 8) // 2
                    pe.wait_ge(f_u, PAIRS * c.k + 2 * h + 2)
                    if c.first() and h == 0:
                        pe.wait_ge(folded, 1)
                    for tt in range(TT):
                        free(c, tt, 3 + h)
                        for j in range(HB):
                            last = mm(fp[tt][:, j * P:(j + 1) * P], ub[:, HB * h + j, tt * P:(tt + 1) * P],
                                      diag_d[:, HB * h + j, :])
                        last.then_inc(f_full[tt], 1)
                if n == 11:
                    free(c, 0, 5)
                    for tt in range(TT):
                        for i in range(DB):
                            last = mm(fp[0][:, tt * XP:(tt + 1) * XP], ub[:, i, tt * P:(tt + 1) * P], wx[:, i, :],
                                      i == 0, i == DB - 1)
                    last.then_inc(f_full[0], 1)
                if n == 12:
                    pe.wait_ge(f_bc, c.k + 1)
                    free(c, 1, 5)
                    for tt in range(TT):
                        nc.tensor.transpose(fp[1][0:R, tt * P:(tt + 1) * P], dtn[:, tt, :], ident[:])
                        last = nc.tensor.transpose(fp[1][0:NS, T + tt * P:T + (tt + 1) * P], bn[:, tt, :], ident[:])
                    last.then_inc(f_full[1], 1)
                if n in (13, 14):
                    if n == 13:
                        pe.wait_ge(f_used[1], USES * c.k + 6)
                    for b in range(2):
                        i = 2 * (n - 13) + b
                        free(c, b, 6 + n - 13)
                        for j in range(2):
                            last = mm(two(fp[b])[:, j, :], wdt[:, (2 * i + j) * P:(2 * i + j + 1) * P], dt_t[:])
                        last.then_inc(f_full[b], 1)

            def scan(c, n, prev):
                for h in range(2):
                    item = ITEMS * c.k + 2 * n + h
                    pe.wait_ge(scan_done, 2 * item + 2)
                    for tt in range(TT):
                        if n or h or c.later(1):
                            pe.wait_ge(y_added, 2 * item + tt - 1)
                        for j in range(HB):
                            last = nc.tensor.transpose(stt[tt][:, j * P:(j + 1) * P],
                                                       st[h][:, j, tt * P:(tt + 1) * P], ident[:])
                        last.then_inc(st_turned, 1)

            def back(c, n):
                if n < PAIRS:
                    i = n
                    if i == 0:
                        pe.wait_ge(y_added, BANKS * c.k + BANKS)
                    rfree(c, i % 2, GATE_USES + i // 2)
                    for j in range(2):
                        for tt in range(TT):
                            last = nc.tensor.transpose(
                                two(bp[i % 2])[:, j, tt * P:(tt + 1) * P],
                                acc[c.par][:, tt, (2 * i + j) * P:(2 * i + j + 1) * P], ident[:])
                    last.then_inc(r_full[i % 2], 1)
                if n == 5:
                    pe.wait_ge(r_used[0], USES * c.k + GATE_USES + 2)
                    pe.wait_ge(r_used[1], USES * c.k + GATE_USES + 2)
                    if c.first():
                        pe.wait_ge(folded, 3)
                    for tt in range(TT):
                        for i in range(DB):
                            last = mm(bp[tt][:, :], y[:, i, tt * P:(tt + 1) * P], wout[:, i, :], i == 0, i == DB - 1)
                        last.then_inc(r_full[tt], 1)
                if n == 7:
                    pe.wait_ge(r_xn, c.k + 1)
                    for b in range(2):
                        rfree(c, b, GATE_USES + 3)
                        for j in range(2):
                            for tt in range(TT):
                                last = nc.tensor.transpose(
                                    two(bp[b])[:, j, tt * P:(tt + 1) * P],
                                    x2[:, tt, (2 * b + j) * P:(2 * b + j + 1) * P], ident[:])
                        last.then_inc(r_full[b], 1)
                if n == 8:
                    pe.wait_ge(r_used[0], USES * c.k + GATE_USES + 4)
                    pe.wait_ge(r_used[1], USES * c.k + GATE_USES + 4)
                    for tt in range(TT):
                        for q in range(KT):
                            mm(bp[tt][:, :], h2t[:, q, tt * P:(tt + 1) * P], fw[:, q, :], q == 0, False)
                        mm(bp[tt][:, :], ones[0:1, :], fb[:], False, True).then_inc(r_full[tt], 1)
                if n == 9:
                    rfree(c, 0, GATE_USES + 5)
                    for tt in range(TT):
                        for q in range(KT):
                            mm(bp[0][:, tt * E:(tt + 1) * E], h2t[:, q, tt * P:(tt + 1) * P], fw8[:, q, :], q == 0, False)
                        mm(bp[0][:, tt * E:(tt + 1) * E], ones[0:1, :], fb8[:], False, True)
                    for q in range(KT):
                        last = mm(bp[0][0:RANK, T:2 * T], fa[:, q, :], h2t[:, q, :], q == 0, q == KT - 1)
                    last.then_inc(r_full[0], 1)
                if n == 10:
                    pe.wait_ge(r_used[0], USES * c.k + GATE_USES + 6)
                    rfree(c, 1, GATE_USES + 5)
                    for tt in range(TT):
                        last = mm(bp[1][:, tt * E:(tt + 1) * E], zk[:, tt * P:(tt + 1) * P], limt[:])
                    last.then_inc(r_full[1], 1)

            def gates(c, n):
                if 11 <= n < 11 + PAIRS:
                    i = n - 11
                    if c.first() and i == 0:
                        pe.wait_ge(w_loaded[2], 16)
                    rfree(c, i % 2, i // 2)
                    for j in range(2):
                        for q in range(KT):
                            last = mm(two(bp[i % 2])[:, j, :], win[:, q, D + (2 * i + j) * P:D + (2 * i + j + 1) * P],
                                      ht_in[c.par][:, q, :], q == 0, q == KT - 1)
                    last.then_inc(r_full[i % 2], 1)

            last_c = over_chunks(pe, front, scan, back, gates)
            for n in range(NS):
                back(last_c, n)
            pe.wait_ge(t_link, TAIL_W)
            pe.wait_ge(f_used[0], USES * NC)
            pe.wait_ge(f_used[1], USES * NC)
            banks = [fp[0], fp[1], decay[0], decay[1]]
            for q in range(4):
                for i in range(4):
                    last = nc.tensor.transpose(banks[q][0:E, i * P:(i + 1) * P], tw[0][:, 4 * q + i, :], ident[:])
                last.then_inc(t_pe, 1)
            pbanks = [bp[0], bp[1], stt[0], stt[1]]
            pe.wait_ge(r_used[0], USES * NC)
            pe.wait_ge(r_used[1], USES * NC)
            for q in range(4):
                pe.wait_ge(t_act, TAIL_WT + q + 1)
                mm(pbanks[q][0:RANK, :], lim[:], wt_all[q]).then_inc(t_pe, 1)
            for i in range(L // P):
                if i % 4 == 0:
                    pe.wait_ge(t_link, TAIL_W + i // 4 + 1)
                if i >= 4:
                    pe.wait_ge(out_ready, i - 3)
                mm(banks[i % 4][:, :], zall[:, i * P:(i + 1) * P], bm[:]).then_inc(t_pe, 1)


        @block.scalar
        def _(act):
            A = nc.scalar.activation
            nc.scalar.preload_act_table_set("natural_log_exp_and_others")
            act.wait_ge(mod_loaded, 16 * 7)
            A(cnt[:, 0, :], cnd[:], ACT.Exp, scale=-1.0).then_inc(cond_e, 1)
            act.wait_ge(mod_full, 2)
            for g in range(2):
                A(gbc[:, g, :], fp[g][:, :], ACT.Abs).then_inc(mod_abs, 1)
            act.wait_ge(w_loaded[0], w_all[0])
            act.wait_ge(mod_made, 2)
            flink = Links(act, f_alink, F_ALINKS)
            rlink = Links(act, r_alink, R_ALINKS)
            glink = Links(act, g_alink, G_ALINKS)

            def front(c, n):
                k = c.k
                if n == 0:
                    act.wait_ge(f_var, k + 1)
                    flink(c, A(frs[:, :, 0], fmv[:, :, 1], ACT.Ln))
                    A(frs[:, :, 0], frs[:, :, 0], ACT.Exp, scale=-0.5).then_inc(f_rstd, 1)
                if n == 2:
                    if c.later(2):
                        for b in range(2):
                            act.wait_ge(r_full[b], USES * (k - 2) + GATE_USES)
                    for b in range(2):
                        act.wait_ge(f_full[b], USES * k + 1)
                        for j in range(2):
                            q = 2 * b + j
                            last = A(ht_in[c.par][:, q, :], two(fp[b])[:, j, :], ACT.Identity,
                                     scale=mcol[:, 1, q:q + 1], bias=mcol[:, 0, q:q + 1])
                        last.then_inc(f_used[b], 1)
                if 3 <= n < 3 + PAIRS:
                    i = n - 3
                    act.wait_ge(f_full[i % 2], USES * k + 2 + i // 2)
                    if c.later(1):
                        act.wait_ge(f_conv, PAIRS * (k - 1) + i + 1)
                    else:
                        act.wait_ge(const_made, 3)
                    A(upre[:, 2 * i:2 * i + 2, K - 1:], two(fp[i % 2]), ACT.Copy).then_inc(f_used[i % 2], 1)
                if 5 <= n < 5 + PAIRS:
                    i = n - 5
                    act.wait_ge(f_conv, PAIRS * k + i + 1)
                    if i >= 2 or c.later(1):
                        act.wait_ge(f_u, PAIRS * k + i - 1)
                    flink(c, A(se[i % 2][:], ub[:, 2 * i:2 * i + 2, :], ACT.Exp, scale=-1.0))
                    A(se[i % 2][:], se[i % 2][:], ACT.Identity, bias=1.0).then_inc(f_e, 1)
                if n in (9, 11):
                    h = (n - 9) // 2
                    for tt in range(TT):
                        act.wait_ge(f_full[tt], USES * k + 4 + h)
                        A(acc[c.par][:, tt, h * 512:(h + 1) * 512], fp[tt][:, :], ACT.Copy).then_inc(f_used[tt], 1)
                if n == 12:
                    act.wait_ge(f_ms, k + 1)
                    flink(c, A(mr[:], ms[:], ACT.Ln))
                    A(mr[:], mr[:], ACT.Exp, scale=-0.5).then_inc(f_mrstd, 1)
                if n == 13:
                    act.wait_ge(f_full[1], USES * k + 6)
                    if c.later(1):
                        act.wait_ge(f_full[1], USES * k)
                        act.wait_ge(b_out, 16 * k)
                    A(dt_t[:], fp[1][0:R, 0:T], ACT.Copy)
                    A(b_t[:], fp[1][0:NS, T:2 * T], ACT.Copy).then_inc(f_used[1], 1)
                if n in (14, 15):
                    for b in range(2):
                        i = 2 * (n - 14) + b
                        dl, e = delta[c.par], du[c.par]
                        act.wait_ge(f_full[b], USES * k + 7 + n - 14)
                        if c.later(2):
                            act.wait_ge(decay_ready, BANKS * (k - 1))
                            act.wait_ge(drive_ready, ITEMS * (k - 1))
                        for j in range(2):
                            m = 2 * i + j
                            A(e[:, m, :], two(fp[b])[:, j, :], ACT.Abs, bias=dtb[:, m:m + 1])
                            last = A(dl[:, m, :], two(fp[b])[:, j, :], ACT.Relu, bias=dtb[:, m:m + 1])
                        last.then_inc(f_used[b], 1)
                        act.wait_ge(f_used[b], USES * k + 7 + n - 14)
                        s = slice(2 * i, 2 * i + 2)
                        flink(c, A(e[:, s, :], e[:, s, :], ACT.Exp, scale=-1.0))
                        A(e[:, s, :], e[:, s, :], ACT.Ln, bias=1.0).then_inc(f_ln, 1)
                if n == NS - 1:
                    flink.close(c)

            def scan(c, n, prev):
                for h in range(2):
                    if n == 0:
                        act.wait_ge(f_du, PAIRS * c.k + 2 * h + 2)
                    for b in range(2):
                        bankno = BANKS * c.k + 4 * n + 2 * h + b
                        if n or h or c.later(1):
                            act.wait_ge(scan_done, bankno - 1)
                        for j in range(2):
                            m = HB * h + 2 * b + j
                            last = A(two(decay[b])[:, j, :], delta[c.par][:, m, :], ACT.Exp,
                                     scale=an[:, n, m:m + 1])
                        last.then_inc(decay_ready, 1)

            def back(c, n):
                k = c.k
                if n == 6:
                    act.wait_ge(r_var, k + 1)
                    rlink(c, A(brs[:, :, 0], bmv[:, :, 1], ACT.Ln))
                    A(brs[:, :, 0], brs[:, :, 0], ACT.Exp, scale=-0.5).then_inc(r_rstd, 1)
                if n == 8:
                    for b in range(2):
                        act.wait_ge(r_full[b], USES * k + GATE_USES + 4)
                        for j in range(2):
                            q = 2 * b + j
                            last = A(h2t[:, q, :], two(bp[b])[:, j, :], ACT.Identity,
                                     scale=mcol[:, 3, q:q + 1], bias=mcol[:, 2, q:q + 1])
                        last.then_inc(r_used[b], 1)
                if n == 10:
                    act.wait_ge(r_full[0], USES * k + GATE_USES + 6)
                    if c.later(1):
                        act.wait_ge(r_full[1], USES * k)
                    A(hs[:, bass.ds(TT * k, TT), :], bp[0][:, 0:TT * E].rearrange("p (a b) -> p a b", a=TT), ACT.Copy)
                    A(zall[:, bass.ds(T * k, T)], bp[0][0:RANK, T:2 * T], ACT.Copy)
                    A(zk[:], bp[0][0:RANK, T:2 * T], ACT.Copy).then_inc(r_used[0], 1)
                if n == 11:
                    act.wait_ge(r_full[1], USES * k + GATE_USES + 6)
                    A(ds[:, bass.ds(TT * k, TT), :], bp[1][:, 0:TT * E].rearrange("p (a b) -> p a b", a=TT),
                      ACT.Copy).then_inc(r_used[1], 1)
                    rlink.close(c)

            def gates(c, n):
                if 12 <= n < 12 + PAIRS:
                    i, k = n - 12, c.k
                    act.wait_ge(r_full[i % 2], USES * k + i // 2 + 1)
                    s = slice(2 * i, 2 * i + 2)
                    glink(c, A(y[:, s, :], two(bp[i % 2]), ACT.Exp, scale=-1.0))
                    A(y[:, s, :], y[:, s, :], ACT.Identity, bias=1.0).then_inc(g_e, 1)
                if n == 15:
                    glink.close(c)

            last_c = over_chunks(act, front, scan, back, gates)
            for n in range(NS):
                back(last_c, n)
            act.wait_ge(r_used[0], USES * NC)
            act.wait_ge(r_used[1], USES * NC)
            A(tw[0][:], hs[:], ACT.Abs, scale=odd[:]).then_inc(t_act, 1)
            A(tw[1][:], ds[:], ACT.Abs, scale=odd[:]).then_inc(t_act, 1)
            act.wait_ge(t_link, 8)
            A(tw[2][:], tw[2][:], ACT.Exp).then_inc(t_act, 1)
            act.wait_ge(t_link, 13)
            A(tw[3][:], tw[3][:], ACT.Exp, scale=-2.0).then_inc(t_act, 1)
            act.wait_ge(t_act, 4)
            A(tw[3][:], tw[3][:], ACT.Identity, bias=1.0).then_inc(t_act, 1)
            banks = [fp[0], fp[1], decay[0], decay[1]]
            for q in range(4):
                act.wait_ge(t_pe, q + 1)
                A(wt_all[q], banks[q][0:E, :], ACT.Copy).then_inc(t_act, 1)

        @block.gpsimd
        def _(gp):
            G = nc.gpsimd
            G.memset(ident[:], 0.0).then_inc(setup_link, 1)
            G.memset(ones[:], 1.0).then_inc(const_made, 1)
            gp.wait_ge(setup_link, 1)
            G.affine_select(out=ident[:], in_=ident[:], compare_op=ALU.not_equal, fill=1.0, base=0,
                            pattern=[[-1, P]], channel_multiplier=1).then_inc(const_made, 1)
            G.memset(upre[:, :, 0:K - 1], 0.0)
            G.memset(carry[:], 0.0).then_inc(const_made, 1)
            gp.wait_ge(const_made, 3)
            gp.wait_ge(w_loaded[0], w_all[0])
            for i in range(DB):
                G.tensor_scalar(diag_d[:, i, :], ident[:], dp[:, i:i + 1], 1.0, ALU.mult, ALU.mult)
            G.tensor_scalar(wdt[:], wdt[:], dtw[:], 1.0, ALU.mult, ALU.mult).then_inc(folded, 1)
            glink = Links(gp, f_glink, F_GLINKS)

            def fold():
                gp.wait_ge(w_loaded[3], w_all[3])
                gp.wait_ge(mod_made, 3)
                G.tensor_copy(fw8[:], fw[:, :, 0:E])
                G.tensor_copy(fb8[:], fb[:, 0:E]).then_inc(folded, 1)
                gp.wait_ge(folded, 2)
                G.tensor_tensor(wout[:], wout[:], gbc[:, 0:1, :].broadcast_to([P, DB, H]), ALU.mult)
                G.tensor_tensor(fw[:], fw[:], gbc[:, 1:2, :].broadcast_to([P, KT, H]), ALU.mult)
                G.tensor_tensor(fb[:], fb[:], gbc[0:1, 1, :], ALU.mult)
                G.tensor_tensor(bm[:], bm[:], gbc[0:RANK, 1, :], ALU.mult).then_inc(folded, 1)

            def front(c, n):
                if n == 15:
                    for i in range(PAIRS):
                        s = slice(2 * i, 2 * i + 2)
                        gp.wait_ge(f_ln, PAIRS * c.k + i + 1)
                        glink(c, G.tensor_tensor(delta[c.par][:, s, :], delta[c.par][:, s, :], du[c.par][:, s, :], ALU.add))
                        G.tensor_tensor(du[c.par][:, s, :], delta[c.par][:, s, :], ub[:, s, :],
                                        ALU.mult).then_inc(f_du, 1)
                    glink.close(c)

            def scan(c, n, prev):
                for h in range(2):
                    item = ITEMS * c.k + 2 * n + h
                    if n % GROUP == 0 and h == 0:
                        g = n // GROUP
                        gp.wait_ge(brow_in[g % 2], 16 * SLOT_LOADS * c.k + 16 * (g // 2) + 16)
                    if n == 0:
                        gp.wait_ge(f_du, PAIRS * c.k + 2 * h + 2)
                    if n or c.later(1):
                        gp.wait_ge(scan_done, 2 * item - 2)
                    G.tensor_tensor(drive[h][:], du[c.par][:, HB * h:HB * (h + 1), :],
                                    brow[(n // GROUP) % 2][:, n % GROUP:n % GROUP + 1, :].broadcast_to([P, HB, T]),
                                    ALU.mult).then_inc(drive_ready, 1)
                    if n or c.later(1):
                        m = n - 1 if n else NS - 1
                        G.tensor_copy(carry[:, m, HB * h:HB * (h + 1)], st[h][:, :, T - 1]).then_inc(carry_saved, 1)

            def scan0(c, n, prev):
                scan(c, n, prev)
                if c.first() and n == 3:
                    fold()

            last_c = over_chunks(gp, front, scan0, nothing, nothing)
            gp.wait_ge(t_link, 2)
            G.partition_all_reduce(tmr[:], tmx[:], P, bass.bass_isa.ReduceOp.max).then_inc(t_red, 1)

        @block.vector
        def _(dve):
            V = nc.vector
            steps = [0]

            def link0(ins):
                steps[0] += 1
                ins.then_inc(setup_v, 1)
                dve.wait_ge(setup_v, steps[0])

            dve.wait_ge(const_made, 3)
            link0(V.reduce_sum(odd[:], ident[:].rearrange("p (a b) -> p b a", b=2)[:, 1, :], AX))
            dve.wait_ge(cond_e, 1)
            link0(V.tensor_scalar(cnt[:, 0, :], cnt[:, 0, :], 1.0, None, ALU.add))
            link0(V.reciprocal(cnt[:, 0, :], cnt[:, 0, :]))
            V.tensor_tensor(cnt[:, 1, :], cnt[:, 0, :], cnd[:], ALU.mult).then_inc(cond_u, 1)
            dve.wait_ge(cond_u, 1)
            for q in range(KT):
                last = V.tensor_scalar(cbc[:, q, :], ones[:], cnt[:, 1, q:q + 1], None, ALU.mult)
            last.then_inc(cond_bc, 1)
            dve.wait_ge(mod_full, 2)
            mv = bp[0][:, 0:4 * KT].rearrange("p (g m) -> p g m", g=4)
            V.tensor_copy(mcol[:], mv).then_inc(mod_made, 1)
            dve.wait_ge(mod_made, 1)
            for g in (1, 3):
                last = V.tensor_scalar(mcol[:, g, :], mcol[:, g, :], 1.0, None, ALU.add)
            last.then_inc(mod_made, 1)
            dve.wait_ge(mod_abs, 2)
            for g in range(2):
                V.tensor_scalar(gbc[:, g, :], gbc[:, g, :], 0.25, None, ALU.max)
                link0(V.tensor_scalar(x2[:, g, :], fp[g][:, :], 0.0, 2.0, ALU.is_ge, ALU.mult))
                last = V.scalar_tensor_tensor(gbc[:, g, :], x2[:, g, :], -1.0, gbc[:, g, :], ALU.add, ALU.mult)
            last.then_inc(mod_made, 1)
            flink = Links(dve, f_vlink, F_VLINKS)
            rlink = Links(dve, r_vlink, R_VLINKS)
            glink = Links(dve, g_vlink, G_VLINKS)

            def front(c, n):
                k = c.k
                if n == 0:
                    dve.wait_ge(x_in[c.par], 16 * c.turn + 16)
                    for tt in range(TT):
                        flink(c, V.bn_stats(fst[:, tt, :], xt[c.par][:, tt, :]), tt == TT - 1)
                    V.memset(unused[:], 0.0)
                    for tt in range(TT):
                        flink(c, V.bn_aggr(fmv[:, tt, :], fst[:, tt, :]), tt == TT - 1)
                    V.tensor_scalar(fmv[:, :, 1], fmv[:, :, 1], 1e-5, None, ALU.add).then_inc(f_var, 1)
                if n == 1:
                    dve.wait_ge(f_rstd, k + 1)
                    flink(c, V.scalar_tensor_tensor(frs[:, :, 1], fmv[:, :, 0], -1.0, frs[:, :, 0], ALU.mult, ALU.mult))
                    for tt in range(TT):
                        last = V.tensor_scalar(xt[c.par][:, tt, :], xt[c.par][:, tt, :], frs[:, tt, 0:1],
                                               frs[:, tt, 1:2], ALU.mult, ALU.add)
                    last.then_inc(f_xn, 1)
                if 4 <= n < 4 + PAIRS:
                    i = n - 4
                    dve.wait_ge(f_used[i % 2], USES * k + 2 + i // 2)
                    if c.later(1):
                        dve.wait_ge(f_du, PAIRS * (k - 1) + i + 1)
                        dve.wait_ge(f_full[0], USES * (k - 1) + 6)
                    elif i == 0:
                        dve.wait_ge(w_loaded[0], w_all[0])
                    for q in range(K):
                        for j in range(2):
                            m = 2 * i + j
                            src = upre[:, m, q:q + T]
                            if q == 0:
                                ins = V.tensor_scalar(ub[:, m, :], src, cw[:, m, 0:1], cb[:, m:m + 1], ALU.mult, ALU.add)
                            else:
                                ins = V.scalar_tensor_tensor(ub[:, m, :], src, cw[:, m, q:q + 1], ub[:, m, :],
                                                             ALU.mult, ALU.add)
                            if j == 1:
                                flink(c, ins)
                    V.tensor_copy(upre[:, 2 * i:2 * i + 2, 0:K - 1], upre[:, 2 * i:2 * i + 2, T:T + K - 1]).then_inc(f_conv, 1)
                if 6 <= n < 6 + PAIRS:
                    i = n - 6
                    s = slice(2 * i, 2 * i + 2)
                    dve.wait_ge(f_e, PAIRS * k + i + 1)
                    flink(c, V.reciprocal(se[i % 2][:], se[i % 2][:]))
                    V.tensor_tensor(ub[:, s, :], ub[:, s, :], se[i % 2][:], ALU.mult).then_inc(f_u, 1)
                if n == 11:
                    dve.wait_ge(f_full[0], USES * k + 6)
                    V.tensor_copy(ssm[:], fp[0][:, 0:TT * XP].rearrange("p (a b) -> p a b", a=TT)).then_inc(f_used[0], 1)
                    dve.wait_ge(f_used[0], USES * k + 6)
                    flink(c, V.tensor_tensor(ssq[:], ssm[:], ssm[:], ALU.mult))
                    V.reduce_sum(ms[:, :, 0], ssq[:, :, 0:R], AX)
                    flink(c, V.reduce_sum(ms[:, :, 1:3], ssq[:, :, R:].rearrange("p a (g b) -> p a g b", g=2), AX))
                    V.tensor_scalar(ms[:, :, 0], ms[:, :, 0], 1.0 / R, 1e-6, ALU.mult, ALU.add)
                    V.tensor_scalar(ms[:, :, 1:3], ms[:, :, 1:3], 1.0 / NS, 1e-6, ALU.mult, ALU.add).then_inc(f_ms, 1)
                if n == 12:
                    dve.wait_ge(f_mrstd, k + 1)
                    if c.later(1):
                        dve.wait_ge(f_full[1], USES * (k - 1) + 6)
                    if c.later(2):
                        dve.wait_ge(y_added, BANKS * (k - 1))
                    for tt in range(TT):
                        V.tensor_scalar(dtn[:, tt, :], ssm[:, tt, 0:R], mr[:, tt, 0:1], None, ALU.mult)
                        V.scalar_tensor_tensor(bn[:, tt, :], ssm[:, tt, R:R + NS], mr[:, tt, 1:2], bw[:],
                                               ALU.mult, ALU.mult)
                        last = V.scalar_tensor_tensor(cn[c.par][:, tt, :], ssm[:, tt, R + NS:], mr[:, tt, 2:3],
                                                      cwt[:], ALU.mult, ALU.mult)
                    last.then_inc(f_bc, 1)
                    flink.close(c)

            def add_states(k, par, n, h):
                item = ITEMS * k + 2 * n + h
                for tt in range(TT):
                    dve.wait_ge(st_turned, 2 * item + tt + 1)
                    if n:
                        dve.wait_ge(y_added, 2 * item + tt - 3)
                    else:
                        dve.wait_ge(f_used[tt], USES * k + 4 + h)
                        dve.wait_ge(f_bc, k + 1)
                    o = acc[par][:, tt, h * 512:(h + 1) * 512]
                    V.scalar_tensor_tensor(o, stt[tt][:, :], cn[par][:, tt, n:n + 1], o, ALU.mult,
                                           ALU.add).then_inc(y_added, 1)

            def scan(c, n, prev):
                for h in range(2):
                    item = ITEMS * c.k + 2 * n + h
                    dve.wait_ge(drive_ready, item + 1)
                    if n or c.later(1):
                        dve.wait_ge(st_turned, 2 * item - 2)
                        dve.wait_ge(carry_saved, item - 1)
                    elif h == 0:
                        dve.wait_ge(const_made, 3)
                    for b in range(2):
                        dve.wait_ge(decay_ready, 2 * item + b + 1)
                        for j in range(2):
                            m = 2 * b + j
                            last = V.tensor_tensor_scan(st[h][:, m, :], two(decay[b])[:, j, :], drive[h][:, m, :],
                                                        carry[:, n, HB * h + m:HB * h + m + 1], ALU.mult, ALU.add)
                        last.then_inc(scan_done, 1)
                    if h:
                        add_states(c.k, c.par, n, 0)
                    elif n:
                        add_states(c.k, c.par, n - 1, 1)
                    elif c.later(1):
                        add_states(c.k - 1, 1 - c.par, NS - 1, 1)

            def back(c, n):
                k = c.k
                if 1 <= n < 1 + PAIRS:
                    i = n - 1
                    dve.wait_ge(r_full[i % 2], USES * k + GATE_USES + i // 2 + 1)
                    s = slice(2 * i, 2 * i + 2)
                    V.tensor_tensor(y[:, s, :], two(bp[i % 2]), y[:, s, :], ALU.mult).then_inc(r_used[i % 2], 1)
                if n == 6:
                    dve.wait_ge(xr_in, 16 * k + 16)
                    for tt in range(TT):
                        dve.wait_ge(r_full[tt], USES * k + GATE_USES + 3)
                        V.tensor_tensor(xr[:, tt, :], bp[tt][:, :], xr[:, tt, :], ALU.add).then_inc(r_used[tt], 1)
                    for tt in range(TT):
                        dve.wait_ge(r_used[tt], USES * k + GATE_USES + 3)
                        rlink(c, V.bn_stats(bst[:, tt, :], xr[:, tt, :]), tt == TT - 1)
                    V.memset(unused[:], 0.0)
                    for tt in range(TT):
                        rlink(c, V.bn_aggr(bmv[:, tt, :], bst[:, tt, :]), tt == TT - 1)
                    V.tensor_scalar(bmv[:, :, 1], bmv[:, :, 1], 1e-5, None, ALU.add).then_inc(r_var, 1)
                    dve.wait_ge(r_rstd, k + 1)
                    rlink(c, V.scalar_tensor_tensor(brs[:, :, 1], bmv[:, :, 0], -1.0, brs[:, :, 0], ALU.mult, ALU.mult))
                    for tt in range(TT):
                        last = V.tensor_scalar(x2[:, tt, :], xr[:, tt, :], brs[:, tt, 0:1], brs[:, tt, 1:2],
                                               ALU.mult, ALU.add)
                    last.then_inc(r_xn, 1)
                if n == 9:
                    for tt in range(TT):
                        dve.wait_ge(r_full[tt], USES * k + GATE_USES + 5)
                        V.tensor_tensor(xr[:, tt, :], bp[tt][:, :], xr[:, tt, :], ALU.add).then_inc(r_used[tt], 1)
                    rlink.close(c)

            def gates(c, n):
                for i in {13: (0,), 14: (1,), 15: (2, 3)}.get(n, ()):
                    s = slice(2 * i, 2 * i + 2)
                    dve.wait_ge(g_e, PAIRS * c.k + i + 1)
                    glink(c, V.reciprocal(y[:, s, :], y[:, s, :]))
                    V.tensor_tensor(y[:, s, :], two(bp[i % 2]), y[:, s, :], ALU.mult).then_inc(r_used[i % 2], 1)
                if n == 15:
                    glink.close(c)

            last_c = over_chunks(dve, front, scan, back, gates)
            add_states(NC - 1, 1, NS - 1, 1)
            for n in range(NS):
                back(last_c, n)

            t = [0]

            def tl(ins):
                t[0] += 1
                ins.then_inc(t_link, 1)
                dve.wait_ge(t_link, t[0])

            def each(v):
                return v[:, :, None].broadcast_to([P, lt, E])

            dve.wait_ge(t_act, 2)
            tl(V.reduce_max(tmx[:, 0:1], tw[0][:].rearrange("p a b -> p (a b)"), AX))
            tl(V.reduce_max(tmx[:, 1:2], tw[1][:].rearrange("p a b -> p (a b)"), AX))
            dve.wait_ge(t_red, 1)
            tl(V.tensor_scalar(tmr[:], tmr[:], 1e-6, 2.0, ALU.max, ALU.mult))
            tl(V.reciprocal(tmr[:], tmr[:]))
            tl(V.tensor_scalar(tw[2][:], ds[:], tmr[:, 1:2], None, ALU.mult))
            tl(V.scalar_tensor_tensor(tw[2][:], hs[:], tmr[:, 0:1], tw[2][:], ALU.mult, ALU.add))
            tl(V.reduce_max(tm[:, 0, :], tw[2][:], AX))
            tl(V.tensor_tensor(tw[2][:], tw[2][:], each(tm[:, 0, :]), ALU.subtract))
            dve.wait_ge(t_act, 3)
            tl(V.reduce_sum(tm[:, 1, :], tw[2][:], AX))
            tl(V.reciprocal(tm[:, 1, :], tm[:, 1, :]))
            tl(V.tensor_tensor(tw[2][:], tw[2][:], each(tm[:, 1, :]), ALU.mult))
            for i in range(lt):
                last = V.max(tw[4][:, i, :], tw[2][:, i, :])
            tl(last)
            tl(V.tensor_tensor(tw[3][:], tw[2][:], each(tw[4][:, :, 1]), ALU.subtract))
            dve.wait_ge(t_act, 5)
            tl(V.reciprocal(tw[3][:], tw[3][:]))
            tl(V.tensor_tensor(tw[2][:], tw[2][:], tw[3][:], ALU.mult))
            tl(V.reduce_sum(tm[:, 2, :], tw[2][:], AX))
            tl(V.tensor_scalar(tm[:, 2, :], tm[:, 2, :], 1e-9, None, ALU.add))
            tl(V.reciprocal(tm[:, 2, :], tm[:, 2, :]))
            tl(V.tensor_tensor(tw[0][:], tw[2][:], each(tm[:, 2, :]), ALU.mult))
            assert t[0] == TAIL_W, t[0]
            pbanks = [bp[0], bp[1], stt[0], stt[1]]
            for q in range(4):
                dve.wait_ge(t_pe, 4 + q + 1)
                z = zall[:, q * 512:(q + 1) * 512].rearrange("p (a b) -> p a b", b=2)
                pm = pbanks[q][0:RANK, :].rearrange("p (a b) -> p a b", b=2)[:, :, 1:2].broadcast_to([RANK, 256, 2])
                V.scalar_tensor_tensor(z, z, 0.5, pm, ALU.mult, ALU.mult).then_inc(t_link, 1)
            dve.wait_ge(base_in, 16 * len(base_tiles))
            banks = [fp[0], fp[1], decay[0], decay[1]]
            for i in range(lt):
                dve.wait_ge(t_pe, 8 + i + 1)
                o = base_tiles[i // 4][:, i % 4, :]
                V.tensor_tensor(o, banks[i % 4][:, :], o, ALU.add).then_inc(out_ready, 1)



INS = ["x", "w_in", "conv_w", "conv_b", "w_x", "dt_w", "b_w", "c_w", "w_dt", "dt_bias", "a_neg", "d_par", "w_out",
       "ffn_w", "ffn_b", "ffn_a", "bmat", "limes", "limes_t", "cond", "wmod"]


def kernel(**inputs):
    import numpy as np
    import concourse.bacc as bacc
    from concourse.bass_utils import run_bass_kernel_spmd as run

    v = {k: np.asarray(a) for k, a in inputs.items()}

    def tiles(a):
        return a.reshape(a.shape[0] // P, P, -1).transpose(1, 0, 2)

    def column(a):
        return a.reshape(-1, P).T

    at = "L0_attn_"
    data = {
        "x": v[at + "hidden_states"],
        "w_in": tiles(v[at + "W_in"].T),
        "conv_w": tiles(v[at + "conv_w"]),
        "conv_b": column(v[at + "conv_b"]),
        "w_x": tiles(v[at + "Wx"].T),
        "dt_w": v[at + "dt_ln_w"][:, None],
        "b_w": v[at + "b_ln_w"],
        "c_w": v[at + "c_ln_w"],
        "w_dt": v[at + "Wdt"].T,
        "dt_bias": column(v[at + "dt_bias"]),
        "a_neg": tiles(v[at + "A"]).transpose(0, 2, 1),
        "d_par": column(v[at + "D_param"]),
        "w_out": tiles(v[at + "W_out"].T),
        "ffn_w": tiles(v["L0_ffn_W"].T),
        "ffn_b": v["L0_ffn_b"][None, :],
        "ffn_a": tiles(v["L0_ffn_A"]),
        "bmat": v["L0_ffn_Bmat"],
        "limes": v["L0_ffn_LiMEs"],
        "limes_t": v["L0_ffn_LiMEs"].T,
        "cond": column(v["L0_c"][0]),
        "wmod": v["L0_wmod"],
    }
    nc = bacc.Bacc("TRN2", target_bir_lowering=False, num_devices=1)
    arrays, args = {}, []
    for name in INS:
        a = np.ascontiguousarray(data[name])
        arrays[name] = a
        args.append(nc.dram_tensor(name, a.shape, mybir.dt.from_np(a.dtype), kind="ExternalInput").ap())
    out = nc.dram_tensor("out", (1, L, H), mybir.dt.float32, kind="ExternalOutput").ap()
    build(nc, *args, out)
    r = run(nc, [arrays], core_ids=[0])
    return r.results[0]["out"]
```

```python
import concourse.bass as bass
from concourse import mybir
from contextlib import ExitStack

L, H, D, NS, R, K = 2048, 512, 1024, 16, 32, 4
E, RANK = 8, 32
P = 128
T = 256
NC = L // T
TT = T // P
DB = D // P
KT = H // P
HB = DB // 2
PAIRS = DB // 2
ITEMS = 2 * NS
BANKS = 2 * ITEMS
RING = 4
SAVE_LAG = 3
EARLY = 8
LATE = 7
ADD_LAG = 2
USES = 8
GROUP = 2
SLOT_LOADS = NS // GROUP // 2
XP = R + 2 * NS


class Chunk:

    def __init__(self, k, turn, par):
        self.k, self.turn, self.par = k, turn, par
        self.links = {}

    def first(self):
        return isinstance(self.k, int) and self.k == 0

    def later(self, n):
        return not isinstance(self.k, int) or self.k >= n


def static(k):
    return Chunk(k, k // 2, k % 2)


def build(nc, x, w_in, conv_w, conv_b, w_x, dt_w, b_w, c_w, w_dt, dt_bias, a_neg, d_par, w_out,
          ffn_w, ffn_b, ffn_a, bmat, limes, limes_t, cond, wmod, out):
    f32 = mybir.dt.float32
    ALU = mybir.AluOpType
    ACT = mybir.ActivationFunctionType
    AX = mybir.AxisListType.X
    with ExitStack() as ctx:
        def sb(name, *shape):
            return ctx.enter_context(nc.sbuf_tensor(name, list(shape), f32))

        def bank(name):
            return ctx.enter_context(nc.psum_tensor(name, [P, 512], f32))

        def sem(name):
            return ctx.enter_context(nc.semaphore(name))

        win = sb("win", P, KT, 2 * D)
        wx = sb("wx", P, DB, XP)
        wdt = sb("wdt", R, D)
        wout = sb("wout", P, DB, H)
        fw = sb("fw", P, KT, H)
        fw16 = sb("fw16", P, KT, 2 * E)
        fa = sb("fa", P, KT, RANK)
        fb = sb("fb", 1, H)
        fb16 = sb("fb16", 1, 2 * E)
        bm = sb("bm", RANK, H)
        lim = sb("lim", E, RANK)
        limt = sb("limt", RANK, E)
        an = sb("an", P, NS, DB)
        cw = sb("cw", P, DB, K)
        cb = sb("cb", P, DB)
        dtb = sb("dtb", P, DB)
        dp = sb("dp", P, DB)
        dtw = sb("dtw", R, 1)
        bw = sb("bw", P, NS)
        cwt = sb("cwt", P, NS)
        cnd = sb("cnd", P, KT)
        cnt = sb("cnt", P, 2, KT)
        mcol = sb("mcol", P, 4, KT)
        ident = sb("ident", P, P)
        ones = sb("ones", P, P)
        diag_d = sb("diag_d", P, DB, P)
        odd = sb("odd", P, 1)
        xt = [sb(f"xt{i}", P, TT, H) for i in range(2)]
        ht_in = [sb(f"ht_in{i}", P, KT, T) for i in range(2)]
        upre = sb("upre", P, DB, K - 1 + T)
        ub = sb("ub", P, DB, T)
        se = [sb(f"se{i}", P, 2, T) for i in range(2)]
        unused = sb("unused", P, 1)
        fst = sb("fst", P, TT, 6)
        fmv = sb("fmv", P, TT, 2)
        frs = sb("frs", P, TT, 2)
        ssm = sb("ssm", P, TT, XP)
        ssq = sb("ssq", P, TT, XP)
        ms = sb("ms", P, TT, 3)
        mr = sb("mr", P, TT, 3)
        dtn = sb("dtn", P, TT, R)
        bn = sb("bn", P, TT, NS)
        cn = [sb(f"cn{i}", P, TT, NS) for i in range(2)]
        dt_t = sb("dt_t", R, T)
        b_t = sb("b_t", NS, T)
        delta = [sb(f"delta{i}", P, DB, T) for i in range(2)]
        du = [sb(f"du{i}", P, DB, T) for i in range(2)]
        brow = [sb(f"brow{i}", P, GROUP, T) for i in range(2)]
        decay = [sb(f"decay{i}", P, HB, 1 + T) for i in range(2)]
        st = [sb(f"st{i}", P, HB, 1 + T) for i in range(RING)]
        carry = sb("carry", P, NS, DB)
        acc = [sb(f"acc{i}", P, TT, D) for i in range(2)]
        y = sb("y", P, DB, T)
        ge = [sb(f"ge{i}", P, 2, T) for i in range(2)]
        xr = sb("xr", P, TT, H)
        x2 = xt
        h2t = [t[:].rearrange("p a h -> p (a h)").rearrange("p (q t) -> p q t", q=KT) for t in xt]
        cbc = ge[0][:].rearrange("p a t -> p (a t)").rearrange("p (k m) -> p k m", k=KT)
        gbc = xr
        fa_t = ge[1][0:RANK, :, :].rearrange("p a t -> p (a t)")
        bst = sb("bst", P, TT, 6)
        bmv = sb("bmv", P, TT, 2)
        brs = sb("brs", P, TT, 2)
        zk = sb("zk", RANK, T)
        hd = sb("hd", P, L // P, 2 * E)
        hs, ds = hd[:, :, 0:E], hd[:, :, E:2 * E]
        lt = L // P
        tw = [st[0][:].rearrange("p a t -> p (a t)")[:, i * lt * E:(i + 1) * lt * E]
              .rearrange("p (a b) -> p a b", b=E) for i in range(5)]
        zall = y[0:RANK, :, :].rearrange("p a t -> p (a t)")
        tmx = sb("tmx", P, 2)
        tmr = sb("tmr", P, 2)
        tm = st[1][:].rearrange("p a t -> p (a t)")[:, 0:3 * lt].rearrange("p (a b) -> p a b", b=lt)

        b_dram = nc.dram_tensor("b_rows", [2, NS, T], f32, kind="Internal").ap()
        base_dram = nc.dram_tensor("base", [L, H], f32, kind="Internal").ap()

        z_dram = nc.dram_tensor("z", [RANK, L], f32, kind="Internal").ap()

        stt = [bank(f"stt{i}") for i in range(2 * TT)]
        fp = [bank(f"fp{i}") for i in range(2)]
        bp = [bank(f"bp{i}") for i in range(2)]

        def nothing(c, p):
            pass

        def two(b):
            return (b if isinstance(b, bass.AP) else b[:, :]).rearrange("p (a t) -> p a t", a=2)

        w_loaded = [sem(f"w_loaded{i}") for i in range(4)]
        cond_loaded = sem("cond_loaded")
        mod_loaded = [sem(f"mod_loaded{i}") for i in range(2)]
        fa_pe = sem("fa_pe")
        fa_act = sem("fa_act")
        const_made = sem("const_made")
        cond_e = sem("cond_e")
        cond_u = sem("cond_u")
        cond_bc = sem("cond_bc")
        mod_full = sem("mod_full")
        mod_abs = sem("mod_abs")
        mod_made = sem("mod_made")
        folded = sem("folded")
        setup_link = sem("setup_link")
        setup_v = sem("setup_v")
        x_in = [sem(f"x_in{i}") for i in range(2)]
        f_full = [sem(f"f_full{i}") for i in range(2)]
        f_used = [sem(f"f_used{i}") for i in range(2)]
        f_var = sem("f_var")
        f_rstd = sem("f_rstd")
        f_xn = sem("f_xn")
        f_tap = sem("f_tap")
        f_conv = sem("f_conv")
        f_s = sem("f_s")
        f_u = sem("f_u")
        f_ms = sem("f_ms")
        f_mrstd = sem("f_mrstd")
        f_bc = sem("f_bc")
        f_ln = sem("f_ln")
        f_du = sem("f_du")
        n_vlink = sem("n_vlink")
        n_alink = sem("n_alink")
        f_vlink = sem("f_vlink")
        f_alink = sem("f_alink")
        f_glink = sem("f_glink")
        b_out = sem("b_out")
        brow_in = [sem(f"brow_in{i}") for i in range(2)]
        decay_ready = sem("decay_ready")
        scan_done = sem("scan_done")
        drive_ready = sem("drive_ready")
        carry_saved = sem("carry_saved")
        st_turned = sem("st_turned")
        y_added = sem("y_added")
        r_full = [sem(f"r_full{i}") for i in range(2)]
        r_used = [sem(f"r_used{i}") for i in range(2)]
        g_y = sem("g_y")
        g_cut = sem("g_cut")
        g_s = sem("g_s")
        g_alink = sem("g_alink")
        xr_in = sem("xr_in")
        r_var = sem("r_var")
        r_rstd = sem("r_rstd")
        r_xn = sem("r_xn")
        r_vlink = sem("r_vlink")
        r_alink = sem("r_alink")
        base_out = sem("base_out")
        z_out = sem("z_out")
        t_link = sem("t_link")
        t_act = sem("t_act")
        t_pe = sem("t_pe")
        t_red = sem("t_red")
        base_in = sem("base_in")
        z_in = sem("z_in")
        out_done = sem("out_done")

        GATE_USES = PAIRS // 2
        Y, ATTN, NORM, LIN, ADAPT = 0, 2, 3, 4, 5

        def before(c, use):
            last = isinstance(c.k, int) and c.k == NC - 1
            gates_between = 0 if last or use < NORM else 1 if use == NORM else 2
            return USES * c.k + GATE_USES + use + gates_between

        def before_gates(c, use):
            return use if c.first() else USES * c.k - 3 + 2 * use

        LEAST = -41.0
        N_VLINKS, N_ALINKS = 3, 1
        F_VLINKS, F_ALINKS, F_GLINKS = 26, 13, 4
        R_VLINKS, R_ALINKS, G_ALINKS = 5, 1, 2 * PAIRS

        class Links:

            def __init__(self, eng, s, per):
                self.eng, self.s, self.per = eng, s, per

            def __call__(self, c, ins, wait=True, n=None):
                if n is None:
                    n = c.links[self.s.name] = c.links.get(self.s.name, 0) + 1
                ins.then_inc(self.s, 1)
                if wait:
                    self.eng.wait_ge(self.s, self.per * c.k + n)

            def close(self, c):
                assert c.links[self.s.name] == self.per, (self.s.name, c.links[self.s.name])

        out_ready = sem("out_ready")
        spots = [delta[0], du[0], delta[1], du[1], acc[1], y]
        base_tiles = [b[:].rearrange("p a b -> p (a b)").rearrange("p (t h) -> p t h", t=4)
                      for b in (delta[0], delta[1], du[0], du[1])]
        w_all = [16 * 10, 16, 16, 16 * 7]
        TAIL_W, TAIL_WT = 19, 5
        wt_all = [ub[0:E, 2 * q:2 * q + 2, :].rearrange("p a b -> p (a b)") for q in range(4)]

        block = ctx.enter_context(nc.Block())

        def over_chunks(eng, front, scan, back, gates, scanned=lambda: None):
            def chunk(prev2, prev, c, nxt, nxt2):
                for p in range(ITEMS):
                    scan(c, p)
                    late(prev2, prev, p)
                    if prev is not None:
                        back(prev, p)
                    if nxt is not None:
                        front(nxt, p)
                    if nxt2 is not None and p >= ITEMS - EARLY:
                        front(nxt2, p - ITEMS)
                    gates(c, p)

            def late(prev2, prev, p):
                if prev2 is not None and p < LATE:
                    back(prev2, ITEMS + p)
                if prev is not None and p < LATE:
                    gates(prev, ITEMS + p)

            for p in range(-EARLY, 0):
                front(static(0), p)
            c0 = static(0)
            for p in range(ITEMS):
                front(c0, p)
                if p >= ITEMS - EARLY:
                    front(static(1), p - ITEMS)

            def at(k):
                return static(k) if 0 <= k < NC else None

            def fixed(k):
                chunk(at(k - 2), at(k - 1), at(k), at(k + 1), at(k + 2))

            fixed(0)
            fixed(1)
            with eng.Fori(0, NC // 2 - 2) as m:
                for j in range(2):
                    chunk(*(Chunk(2 * m + i, m + i // 2, i % 2) for i in range(j, j + 5)))
            fixed(NC - 2)
            fixed(NC - 1)
            scanned()
            last = static(NC - 1)
            for p in range(ITEMS):
                late(static(NC - 2), last, p)
                back(last, p)
            for p in range(LATE):
                back(last, ITEMS + p)

        @block.sync
        def _(sp):
            def load(dst, src, s):
                sp.dma_start(dst, src).then_inc(s, 16)

            def value(e):
                return e if isinstance(e, int) else sp.snap(e)

            load(cnd[:], cond, cond_loaded)
            mods = wmod.rearrange("(k p) (j n) -> j p k n", p=P, j=6)
            for j in (0, 1):
                load(spots[j][:].rearrange("p a b -> p (a b)").rearrange("p (k n) -> p k n", k=KT),
                     mods[j], mod_loaded[0])
            for i in range(2):
                load(xt[i][:], x[0, i * T:(i + 1) * T, :].rearrange("(t p) h -> p t h", p=P), x_in[i])
            load(bw[:], b_w[None, :].broadcast_to([P, NS]), w_loaded[0])
            load(cwt[:], c_w[None, :].broadcast_to([P, NS]), w_loaded[0])
            for dst, src in ((dtw, dt_w), (an, a_neg), (cw, conv_w), (cb, conv_b), (dtb, dt_bias),
                             (dp, d_par), (wx, w_x), (wdt, w_dt)):
                load(dst[:], src, w_loaded[0])
            load(win[:, :, 0:D], w_in[:, :, 0:D], w_loaded[1])
            for j in (2, 3, 4, 5):
                load(spots[j][:].rearrange("p a b -> p (a b)").rearrange("p (k n) -> p k n", k=KT),
                     mods[j], mod_loaded[1])
            load(win[:, :, D:2 * D], w_in[:, :, D:2 * D], w_loaded[2])
            for dst, src in ((wout, w_out), (fw, ffn_w), (fa, ffn_a), (fb, ffn_b), (bm, bmat),
                             (lim, limes), (limt, limes_t)):
                load(dst[:], src, w_loaded[3])

            def front(c, p):
                if p == -8 and c.later(2):
                    if c.later(3):
                        at, done = value(c.k * T), value(before(Chunk(c.k - 3, 0, 0), NORM) + 1)
                        sp.wait_ge(r_full[1], done)
                    else:
                        at = c.k * T
                        sp.wait_ge(f_full[1], 1)
                    load(xt[c.par][:], x[0, bass.ds(at, T), :].rearrange("(t p) h -> p t h", p=P),
                         x_in[c.par])
                if p == 23:
                    sp.wait_ge(f_used[1], USES * c.k + 6)
                    load(b_dram[c.par], b_t[:], b_out)

            def scan(c, p):
                if p == 0:
                    rows(c, 0)
                    rows(c, 1)
                elif p % (2 * GROUP) == 0 and p + 2 * GROUP < ITEMS:
                    rows(c, p // (2 * GROUP) + 1)

            def rows(c, g):
                if g == 0:
                    sp.wait_ge(b_out, 16 * c.k + 16)
                if g >= 2 or c.later(1):
                    sp.wait_ge(drive_ready, ITEMS * c.k + 2 * GROUP * (g - 1))
                load(brow[g % 2][:], b_dram[c.par, GROUP * g:GROUP * (g + 1), :][None].broadcast_to([P, GROUP, T]),
                     brow_in[g % 2])

            def back(c, p):
                if p == 7:
                    at = value(c.k * T)
                    if c.later(1):
                        sp.wait_ge(base_out, 16 * c.k)
                        sp.wait_ge(z_out, 16 * c.k)
                    else:
                        sp.wait_ge(folded, 3)
                    load(xr[:], x[0, bass.ds(at, T), :].rearrange("(t p) h -> p t h", p=P), xr_in)
                if p == ITEMS + 6:
                    at, done = value(c.k * T), value(before(c, ADAPT) + 1)
                    sp.wait_ge(r_used[1], done)
                    load(base_dram[bass.ds(at, T), :].rearrange("(t p) h -> p t h", p=P), xr[:], base_out)
                    load(z_dram[:, bass.ds(at, T)], zk[:], z_out)

            over_chunks(sp, front, scan, back, nothing)
            sp.wait_ge(z_out, 16 * NC)
            sp.wait_ge(r_full[0], USES * NC)
            load(zall, z_dram, z_in)
            sp.wait_ge(base_out, 16 * NC)
            sp.wait_ge(y_added, BANKS * NC)
            for q, b in enumerate(base_tiles):
                load(b, base_dram[q * 512:(q + 1) * 512, :].rearrange("(t p) h -> p t h", p=P), base_in)
            for q, b in enumerate(base_tiles):
                sp.wait_ge(out_ready, 4 * (q + 1))
                load(out[0, q * 512:(q + 1) * 512, :].rearrange("(t p) h -> p t h", p=P), b, out_done)
            sp.wait_ge(out_done, 16 * len(base_tiles))


        @block.tensor
        def _(pe):
            def mm(o, a, b, start=True, stop=True):
                return nc.tensor.matmul(o, a, b, start=start, stop=stop)

            wm = [s[:].rearrange("p a b -> p (a b)").rearrange("p (k n) -> p k n", k=KT) for s in spots]

            def mod_columns(pieces):
                for g, j in enumerate(pieces):
                    for m in range(KT):
                        for q in range(KT):
                            last = mm(bp[0][:, g * KT + m:g * KT + m + 1], wm[j][:, q, m * P:(m + 1) * P],
                                      cnt[:, 1, q:q + 1], q == 0, q == KT - 1)
                last.then_inc(mod_full, 1)

            def mod_rows(j):
                for q in range(KT):
                    last = mm(bp[1][:, :], cbc[:, q, :], wm[j][:, q, :], q == 0, q == KT - 1)
                last.then_inc(mod_full, 1)

            pe.wait_ge(cond_u, 1)
            pe.wait_ge(mod_loaded[0], 16 * 2)
            mod_columns((0, 1))
            pe.wait_ge(const_made, 3)

            def rest_of_setup(p):
                if p == 1:
                    pe.wait_ge(mod_loaded[1], 16 * 4)
                    pe.wait_ge(mod_made, 1)
                    mod_columns((3, 4))
                    pe.wait_ge(cond_bc, 1)
                    mod_rows(2)
                if p == 5:
                    pe.wait_ge(mod_made, 5)
                    mod_rows(5)
                if p == 10:
                    pe.wait_ge(w_loaded[3], w_all[3])
                    for q in range(KT):
                        last = nc.tensor.transpose(bp[0][0:RANK, q * P:(q + 1) * P], fa[:, q, :], ident[:])
                    last.then_inc(fa_pe, 1)
                if p == 13:
                    pe.wait_ge(fa_act, 1)
                    for q in range(KT):
                        last = mm(bp[0][:, q * E:(q + 1) * E], fa_t[:, q * P:(q + 1) * P], limt[:])
                    last.then_inc(fa_pe, 1)
                if p == 15:
                    pe.wait_ge(fa_act, 2)
                    pe.wait_ge(mod_made, 6)

            def free(c, b, u):
                if u or c.later(1):
                    pe.wait_ge(f_used[b], USES * c.k + u)

            def rfree(b, uses):
                if not isinstance(uses, int) or uses:
                    pe.wait_ge(r_used[b], uses)

            def start_sum(c, h, tt, u):
                free(c, tt, u)
                for j in range(HB):
                    last = mm(fp[tt][:, j * P:(j + 1) * P], ub[:, HB * h + j, tt * P:(tt + 1) * P],
                              diag_d[:, HB * h + j, :])
                last.then_inc(f_full[tt], 1)

            def front(c, p):
                if p == -2:
                    pe.wait_ge(f_xn, c.k + 1)
                    for b in range(2):
                        free(c, b, 0)
                        for j in range(2):
                            for tt in range(TT):
                                last = nc.tensor.transpose(
                                    two(fp[b])[:, j, tt * P:(tt + 1) * P],
                                    xt[c.par][:, tt, (2 * b + j) * P:(2 * b + j + 1) * P], ident[:])
                        last.then_inc(f_full[b], 1)
                if 2 <= p < 2 + DB:
                    i, j = divmod(p - 2, 2)
                    if p == 2:
                        pe.wait_ge(f_used[0], USES * c.k + 1)
                        pe.wait_ge(f_used[1], USES * c.k + 1)
                        if c.first():
                            pe.wait_ge(w_loaded[1], 16)
                    if j == 0:
                        free(c, i % 2, 1 + i // 2)
                    for q in range(KT):
                        last = mm(two(fp[i % 2])[:, j, :], win[:, q, (2 * i + j) * P:(2 * i + j + 1) * P],
                                  ht_in[c.par][:, q, :], q == 0, q == KT - 1)
                    if j:
                        last.then_inc(f_full[i % 2], 1)
                if p == 12:
                    pe.wait_ge(f_u, PAIRS * c.k + 2)
                    if c.first():
                        pe.wait_ge(folded, 1)
                    start_sum(c, 0, 0, 3)
                    start_sum(c, 0, 1, 3)
                if p == 15:
                    pe.wait_ge(f_u, PAIRS * c.k + PAIRS)
                    free(c, 0, 4)
                    for tt in range(TT):
                        for i in range(DB):
                            last = mm(fp[0][:, tt * XP:(tt + 1) * XP], ub[:, i, tt * P:(tt + 1) * P], wx[:, i, :],
                                      i == 0, i == DB - 1)
                    last.then_inc(f_full[0], 1)
                if p == 16:
                    start_sum(c, 1, 1, 4)
                if p == 17:
                    start_sum(c, 1, 0, 5)
                if p == 20:
                    pe.wait_ge(f_bc, c.k + 1)
                    free(c, 1, 5)
                    for tt in range(TT):
                        nc.tensor.transpose(fp[1][0:R, tt * P:(tt + 1) * P], dtn[:, tt, :], ident[:])
                        last = nc.tensor.transpose(fp[1][0:NS, T + tt * P:T + (tt + 1) * P], bn[:, tt, :], ident[:])
                    last.then_inc(f_full[1], 1)
                if 22 <= p < 22 + PAIRS:
                    i = p - 22
                    b = i % 2
                    if i == 0:
                        pe.wait_ge(f_used[1], USES * c.k + 6)
                    free(c, b, 6 + i // 2)
                    for j in range(2):
                        last = mm(two(fp[b])[:, j, :], wdt[:, (2 * i + j) * P:(2 * i + j + 1) * P], dt_t[:])
                    last.then_inc(f_full[b], 1)

            def scan(c, p):
                item, h = ITEMS * c.k + p, p % 2
                pe.wait_ge(scan_done, item + 1)
                for tt in range(TT):
                    if p >= 2 or c.later(1):
                        pe.wait_ge(y_added, 2 * item + tt - 3)
                    for j in range(HB):
                        last = nc.tensor.transpose(stt[TT * h + tt][:, j * P:(j + 1) * P],
                                                   st[p % RING][:, j, 1 + tt * P:1 + (tt + 1) * P], ident[:])
                    last.then_inc(st_turned, 1)

            def back(c, p):
                if 5 <= p < 5 + PAIRS:
                    i = p - 5
                    if i == 0:
                        pe.wait_ge(y_added, BANKS * c.k + BANKS)
                    rfree(i % 2, before(c, Y + i // 2))
                    for j in range(2):
                        for tt in range(TT):
                            last = nc.tensor.transpose(
                                two(bp[i % 2])[:, j, tt * P:(tt + 1) * P],
                                acc[c.par][:, tt, (2 * i + j) * P:(2 * i + j + 1) * P], ident[:])
                    last.then_inc(r_full[i % 2], 1)
                if 10 <= p < 18:
                    if p == 10:
                        rfree(0, before(c, ATTN))
                        rfree(1, before(c, ATTN))
                        if c.first():
                            pe.wait_ge(folded, 3)
                    tt, part = divmod(p - 10, 4)
                    for i in (2 * part, 2 * part + 1):
                        last = mm(bp[tt][:, :], y[:, i, tt * P:(tt + 1) * P], wout[:, i, :], i == 0, i == DB - 1)
                    if part == 3:
                        last.then_inc(r_full[tt], 1)
                if p == 23:
                    pe.wait_ge(r_xn, c.k + 1)
                    for b in range(2):
                        rfree(b, before(c, NORM))
                        for j in range(2):
                            for tt in range(TT):
                                last = nc.tensor.transpose(
                                    two(bp[b])[:, j, tt * P:(tt + 1) * P],
                                    x2[1 - c.par][:, tt, (2 * b + j) * P:(2 * b + j + 1) * P], ident[:])
                        last.then_inc(r_full[b], 1)
                if 29 <= p < 33:
                    tt, part = divmod(p - 29, 2)
                    if part == 0:
                        rfree(tt, before(c, LIN))
                        rfree(1, before(c, NORM) + 1)
                    for q in (2 * part, 2 * part + 1):
                        mm(bp[tt][:, :], h2t[c.par][:, q, tt * P:(tt + 1) * P], fw[:, q, :], q == 0, False)
                    if part:
                        mm(bp[tt][:, :], ones[0:1, :], fb[:], False, True).then_inc(r_full[tt], 1)
                if p == 33:
                    rfree(0, before(c, ADAPT))
                    if c.first():
                        pe.wait_ge(folded, 2)
                    w = 2 * E
                    for tt in range(TT):
                        for q in range(KT):
                            mm(bp[0][:, tt * w:(tt + 1) * w], h2t[c.par][:, q, tt * P:(tt + 1) * P],
                               fw16[:, q, :], q == 0, False)
                        last = mm(bp[0][:, tt * w:(tt + 1) * w], ones[0:1, :], fb16[:], False, True)
                    last.then_inc(r_full[0], 1)
                if p == 35:
                    rfree(1, before(c, ADAPT))
                    for q in range(KT):
                        last = mm(bp[1][0:RANK, 0:T], fa[:, q, :], h2t[c.par][:, q, :], q == 0, q == KT - 1)
                    last.then_inc(r_full[1], 1)

            def gates(c, p):
                if c.first():
                    rest_of_setup(p)
                if p in (16, 17, 20, 21, 25, 26, 27, 28):
                    i, j = divmod((16, 17, 20, 21, 25, 26, 27, 28).index(p), 2)
                    if c.first() and p == 16:
                        pe.wait_ge(w_loaded[2], 16)
                    if j == 0:
                        rfree(i % 2, before_gates(c, i // 2))
                    for q in range(KT):
                        last = mm(two(bp[i % 2])[:, j, :], win[:, q, D + (2 * i + j) * P:D + (2 * i + j + 1) * P],
                                  ht_in[c.par][:, q, :], q == 0, q == KT - 1)
                    if j:
                        last.then_inc(r_full[i % 2], 1)

            over_chunks(pe, front, scan, back, gates)
            pe.wait_ge(t_link, TAIL_W)
            pe.wait_ge(f_used[0], USES * NC)
            pe.wait_ge(f_used[1], USES * NC)
            banks = [fp[0], fp[1], stt[2], stt[3]]
            for q in range(4):
                for i in range(4):
                    last = nc.tensor.transpose(banks[q][0:E, i * P:(i + 1) * P], tw[0][:, 4 * q + i, :], ident[:])
                last.then_inc(t_pe, 1)
            pbanks = [bp[0], bp[1], stt[0], stt[1]]
            rfree(0, USES * NC)
            rfree(1, USES * NC)
            for q in range(4):
                pe.wait_ge(t_act, TAIL_WT + q + 1)
                mm(pbanks[q][0:RANK, :], lim[:], wt_all[q]).then_inc(t_pe, 1)
            for i in range(L // P):
                if i % 4 == 0:
                    pe.wait_ge(t_link, TAIL_W + i // 4 + 1)
                if i >= 4:
                    pe.wait_ge(out_ready, i - 3)
                mm(banks[i % 4][:, :], zall[:, i * P:(i + 1) * P], bm[:]).then_inc(t_pe, 1)


        @block.scalar
        def _(act):
            A = nc.scalar.activation
            nc.scalar.preload_act_table_set("natural_log_exp_and_others")
            act.wait_ge(cond_loaded, 16)
            A(cnt[:, 0, :], cnd[:], ACT.Exp, scale=-1.0).then_inc(cond_e, 1)
            act.wait_ge(w_loaded[0], w_all[0])
            act.wait_ge(mod_made, 2)

            def rest_of_setup(p):
                if p in (3, 7):
                    g = (p - 3) // 4
                    act.wait_ge(mod_full, 3 + g)
                    A(gbc[:, g, :], bp[1][:, :], ACT.Abs).then_inc(mod_abs, 1)
                if p == 12:
                    act.wait_ge(fa_pe, 1)
                    act.wait_ge(mod_made, 6)
                    A(fa_t, bp[0][0:RANK, :], ACT.Copy).then_inc(fa_act, 1)
                if p == 15:
                    act.wait_ge(fa_pe, 2)
                    A(fw16[:, :, E:2 * E], bp[0][:, 0:KT * E].rearrange("p (a b) -> p a b", a=KT),
                      ACT.Copy).then_inc(fa_act, 1)

            nlink = Links(act, n_alink, N_ALINKS)
            flink = Links(act, f_alink, F_ALINKS)
            rlink = Links(act, r_alink, R_ALINKS)
            glink = Links(act, g_alink, G_ALINKS)

            def front(c, p):
                k = c.k
                if p == -3:
                    act.wait_ge(f_var, k + 1)
                    nlink(c, A(frs[:, :, 0], fmv[:, :, 1], ACT.Ln), n=1)
                    A(frs[:, :, 0], frs[:, :, 0], ACT.Exp, scale=-0.5).then_inc(f_rstd, 1)
                if p in (1, 2):
                    b = p - 1
                    if c.later(2) and b == 0:
                        act.wait_ge(r_full[1], before_gates(static(k - 2) if isinstance(k, int) else
                                                            Chunk(k - 2, 0, 0), 1) + 1)
                    act.wait_ge(f_full[b], USES * k + 1)
                    for j in range(2):
                        q = 2 * b + j
                        last = A(ht_in[c.par][:, q, :], two(fp[b])[:, j, :], ACT.Identity,
                                 scale=mcol[:, 1, q:q + 1], bias=mcol[:, 0, q:q + 1])
                    last.then_inc(f_used[b], 1)
                if p in (5, 7, 9, 11):
                    i = (p - 5) // 2
                    act.wait_ge(f_full[i % 2], USES * k + 2 + i // 2)
                    if c.later(1):
                        act.wait_ge(f_conv, PAIRS * (k - 1) + i + 1)
                    else:
                        act.wait_ge(const_made, 3)
                    A(upre[:, 2 * i:2 * i + 2, K - 1:], two(fp[i % 2]), ACT.Copy).then_inc(f_used[i % 2], 1)
                if p in (8, 10, 12, 14):
                    i = (p - 8) // 2
                    act.wait_ge(f_conv, PAIRS * k + i + 1)
                    flink(c, A(se[i % 2][:], se[i % 2][:], ACT.Exp, scale=-1.0))
                    flink(c, A(se[i % 2][:], se[i % 2][:], ACT.Ln, bias=1.0))
                    A(se[i % 2][:], se[i % 2][:], ACT.Exp, scale=-1.0).then_inc(f_s, 1)
                for at, h, tt, use in ((15, 0, 0, 3), (15, 0, 1, 3), (18, 1, 1, 4), (20, 1, 0, 5)):
                    if p == at:
                        act.wait_ge(f_full[tt], USES * k + use + 1)
                        A(acc[c.par][:, tt, h * 512:(h + 1) * 512], fp[tt][:, :], ACT.Copy).then_inc(f_used[tt], 1)
                if p == 19:
                    act.wait_ge(f_ms, k + 1)
                    flink(c, A(mr[:], ms[:], ACT.Ln))
                    A(mr[:], mr[:], ACT.Exp, scale=-0.5).then_inc(f_mrstd, 1)
                if p == 22:
                    act.wait_ge(f_full[1], USES * k + 6)
                    if c.later(1):
                        act.wait_ge(f_full[1], USES * k)
                        act.wait_ge(b_out, 16 * k)
                    A(dt_t[:], fp[1][0:R, 0:T], ACT.Copy)
                    A(b_t[:], fp[1][0:NS, T:2 * T], ACT.Copy).then_inc(f_used[1], 1)
                if 25 <= p < 25 + PAIRS:
                    i = p - 25
                    b = i % 2
                    dl, e = delta[c.par], du[c.par]
                    act.wait_ge(f_full[b], USES * k + 7 + i // 2)
                    if c.later(2):
                        act.wait_ge(decay_ready, ITEMS * (k - 1))
                        act.wait_ge(drive_ready, ITEMS * (k - 1))
                    for j in range(2):
                        m = 2 * i + j
                        A(e[:, m, :], two(fp[b])[:, j, :], ACT.Abs, bias=dtb[:, m:m + 1])
                        last = A(dl[:, m, :], two(fp[b])[:, j, :], ACT.Relu, bias=dtb[:, m:m + 1])
                    last.then_inc(f_used[b], 1)
                    act.wait_ge(f_used[b], USES * k + 7 + i // 2)
                    s = slice(2 * i, 2 * i + 2)
                    flink(c, A(e[:, s, :], e[:, s, :], ACT.Exp, scale=-1.0))
                    A(e[:, s, :], e[:, s, :], ACT.Ln, bias=1.0).then_inc(f_ln, 1)
                if p == ITEMS - 1:
                    flink.close(c)

            def scan(c, p):
                n, h = divmod(p, 2)
                if c.first() and n == 0:
                    act.wait_ge(const_made, 3)
                if n == 0:
                    act.wait_ge(f_du, PAIRS * c.k + 2 * h + 2)
                if p >= 2 or c.later(1):
                    act.wait_ge(scan_done, ITEMS * c.k + p - 1)
                for j in range(HB):
                    m = HB * h + j
                    last = A(decay[h][:, j, 1:], delta[c.par][:, m, :], ACT.Exp, scale=an[:, n, m:m + 1])
                last.then_inc(decay_ready, 1)

            def back(c, p):
                k = c.k
                if p == 21:
                    act.wait_ge(r_var, k + 1)
                    rlink(c, A(brs[:, :, 0], bmv[:, :, 1], ACT.Ln))
                    A(brs[:, :, 0], brs[:, :, 0], ACT.Exp, scale=-0.5).then_inc(r_rstd, 1)
                if p in (25, 26):
                    b = p - 25
                    act.wait_ge(r_full[b], before(c, NORM) + 1)
                    for j in range(2):
                        q = 2 * b + j
                        last = A(h2t[c.par][:, q, :], two(bp[b])[:, j, :], ACT.Identity,
                                 scale=mcol[:, 3, q:q + 1], bias=mcol[:, 2, q:q + 1])
                    last.then_inc(r_used[b], 1)
                if p == 36:
                    act.wait_ge(r_full[0], before(c, ADAPT) + 1)
                    A(hd[:, bass.ds(TT * k, TT), :], bp[0][:, 0:TT * 2 * E].rearrange("p (a b) -> p a b", a=TT),
                      ACT.Copy).then_inc(r_used[0], 1)
                if p == 37:
                    act.wait_ge(r_full[1], before(c, ADAPT) + 1)
                    A(zk[:], bp[1][0:RANK, 0:T], ACT.Copy).then_inc(r_used[1], 1)
                if p == ITEMS - 1:
                    rlink.close(c)

            def gates(c, p):
                k = c.k
                if c.first():
                    rest_of_setup(p)
                if p in (19, 23, 28, 30):
                    i = (19, 23, 28, 30).index(p)
                    s = slice(2 * i, 2 * i + 2)
                    act.wait_ge(r_full[i % 2], before_gates(c, i // 2) + 1)
                    A(y[:, s, :], two(bp[i % 2]), ACT.Copy).then_inc(r_used[i % 2], 1)
                if p in (21, 25, 30, 32):
                    i = (21, 25, 30, 32).index(p)
                    act.wait_ge(g_cut, PAIRS * k + i + 1)
                    glink(c, A(ge[i % 2][:], ge[i % 2][:], ACT.Exp, scale=-1.0), n=2 * i + 1)
                    glink(c, A(ge[i % 2][:], ge[i % 2][:], ACT.Ln, bias=1.0), n=2 * i + 2)
                    A(ge[i % 2][:], ge[i % 2][:], ACT.Exp, scale=-1.0).then_inc(g_s, 1)

            over_chunks(act, front, scan, back, gates)
            act.wait_ge(r_used[0], USES * NC)
            act.wait_ge(r_used[1], USES * NC)
            A(tw[0][:], hs[:], ACT.Abs, scale=odd[:]).then_inc(t_act, 1)
            A(tw[1][:], ds[:], ACT.Abs, scale=odd[:]).then_inc(t_act, 1)
            act.wait_ge(t_link, 8)
            A(tw[2][:], tw[2][:], ACT.Exp).then_inc(t_act, 1)
            act.wait_ge(t_link, 13)
            A(tw[3][:], tw[3][:], ACT.Exp, scale=-2.0).then_inc(t_act, 1)
            act.wait_ge(t_act, 4)
            A(tw[3][:], tw[3][:], ACT.Identity, bias=1.0).then_inc(t_act, 1)
            banks = [fp[0], fp[1], stt[2], stt[3]]
            for q in range(4):
                act.wait_ge(t_pe, q + 1)
                A(wt_all[q], banks[q][0:E, :], ACT.Copy).then_inc(t_act, 1)

        @block.gpsimd
        def _(gp):
            G = nc.gpsimd
            G.memset(ident[:], 0.0).then_inc(setup_link, 1)
            G.memset(ones[:], 1.0).then_inc(const_made, 1)
            gp.wait_ge(setup_link, 1)
            G.affine_select(out=ident[:], in_=ident[:], compare_op=ALU.not_equal, fill=1.0, base=0,
                            pattern=[[-1, P]], channel_multiplier=1).then_inc(const_made, 1)
            G.memset(upre[:, :, 0:K - 1], 0.0)
            for b in decay:
                G.memset(b[:, :, 0:1], 0.0)
            G.memset(fb16[:], 0.0)
            G.memset(carry[:], 0.0).then_inc(const_made, 1)
            gp.wait_ge(const_made, 3)
            gp.wait_ge(w_loaded[0], w_all[0])
            for i in range(DB):
                G.tensor_scalar(diag_d[:, i, :], ident[:], dp[:, i:i + 1], 1.0, ALU.mult, ALU.mult)
            G.tensor_scalar(wdt[:], wdt[:], dtw[:], 1.0, ALU.mult, ALU.mult).then_inc(folded, 1)
            glink = Links(gp, f_glink, F_GLINKS)

            def fold(p):
                if p == 9:
                    gp.wait_ge(w_loaded[3], w_all[3])
                    G.tensor_copy(fw16[:, :, 0:E], fw[:, :, 0:E])
                    G.tensor_copy(fb16[:, 0:E], fb[:, 0:E]).then_inc(folded, 1)
                if 10 <= p < 14:
                    if p == 10:
                        gp.wait_ge(mod_made, 6)
                    s = slice(2 * (p - 10), 2 * (p - 10) + 2)
                    G.tensor_tensor(wout[:, s, :], wout[:, s, :], gbc[:, 0:1, :].broadcast_to([P, 2, H]), ALU.mult)
                if 14 <= p < 16:
                    if p == 14:
                        gp.wait_ge(folded, 2)
                    s = slice(2 * (p - 14), 2 * (p - 14) + 2)
                    G.tensor_tensor(fw[:, s, :], fw[:, s, :], gbc[:, 1:2, :].broadcast_to([P, 2, H]), ALU.mult)
                if p == 16:
                    G.tensor_tensor(fb[:], fb[:], gbc[0:1, 1, :], ALU.mult)
                    G.tensor_tensor(bm[:], bm[:], gbc[0:RANK, 1, :], ALU.mult).then_inc(folded, 1)

            def front(c, p):
                if 27 <= p < 27 + PAIRS:
                    i = p - 27
                    s = slice(2 * i, 2 * i + 2)
                    gp.wait_ge(f_ln, PAIRS * c.k + i + 1)
                    glink(c, G.tensor_tensor(delta[c.par][:, s, :], delta[c.par][:, s, :], du[c.par][:, s, :], ALU.add))
                    G.tensor_tensor(du[c.par][:, s, :], delta[c.par][:, s, :], ub[:, s, :],
                                    ALU.mult).then_inc(f_du, 1)
                if p == ITEMS - 1:
                    glink.close(c)

            def scan(c, p):
                n, h = divmod(p, 2)
                item = ITEMS * c.k + p
                if n % GROUP == 0 and h == 0:
                    g = n // GROUP
                    gp.wait_ge(brow_in[g % 2], 16 * SLOT_LOADS * c.k + 16 * (g // 2) + 16)
                if n == 0:
                    gp.wait_ge(f_du, PAIRS * c.k + 2 * h + 2)
                w = st[p % RING]
                if p >= RING or c.later(1):
                    gp.wait_ge(st_turned, 2 * item - 6)
                    gp.wait_ge(carry_saved, item - 3)
                if p >= SAVE_LAG or c.later(1):
                    gp.wait_ge(scan_done, item - SAVE_LAG + 1)
                G.tensor_tensor(w[:, :, 1:], du[c.par][:, HB * h:HB * (h + 1), :],
                                brow[(n // GROUP) % 2][:, n % GROUP:n % GROUP + 1, :].broadcast_to([P, HB, T]),
                                ALU.mult)
                G.tensor_copy(w[:, :, 0], carry[:, n, HB * h:HB * (h + 1)]).then_inc(drive_ready, 1)
                if p >= SAVE_LAG or c.later(1):
                    m, g = divmod((p - SAVE_LAG) % ITEMS, 2)
                    G.tensor_copy(carry[:, m, HB * g:HB * (g + 1)],
                                  st[(p - SAVE_LAG) % RING][:, :, T]).then_inc(carry_saved, 1)
                if c.first():
                    fold(p)

            over_chunks(gp, front, scan, nothing, nothing)
            gp.wait_ge(t_link, 2)
            G.partition_all_reduce(tmr[:], tmx[:], P, bass.bass_isa.ReduceOp.max).then_inc(t_red, 1)

        @block.vector
        def _(dve):
            V = nc.vector
            steps = [0]

            def link0(ins):
                steps[0] += 1
                ins.then_inc(setup_v, 1)
                dve.wait_ge(setup_v, steps[0])

            dve.wait_ge(const_made, 3)
            link0(V.reduce_sum(odd[:], ident[:].rearrange("p (a b) -> p b a", b=2)[:, 1, :], AX))
            dve.wait_ge(cond_e, 1)
            link0(V.tensor_scalar(cnt[:, 0, :], cnt[:, 0, :], 1.0, None, ALU.add))
            link0(V.reciprocal(cnt[:, 0, :], cnt[:, 0, :]))
            V.tensor_tensor(cnt[:, 1, :], cnt[:, 0, :], cnd[:], ALU.mult).then_inc(cond_u, 1)
            dve.wait_ge(cond_u, 1)
            for q in range(KT):
                last = V.tensor_scalar(cbc[:, q, :], ones[:], cnt[:, 1, q:q + 1], None, ALU.mult)
            last.then_inc(cond_bc, 1)

            def columns(g):
                mv = bp[0][:, 0:2 * KT].rearrange("p (g m) -> p g m", g=2)
                V.tensor_copy(mcol[:, g:g + 2, :], mv).then_inc(mod_made, 1)
                dve.wait_ge(mod_made, 1 if g == 0 else 3)
                V.tensor_scalar(mcol[:, g + 1, :], mcol[:, g + 1, :], 1.0, None, ALU.add).then_inc(mod_made, 1)

            dve.wait_ge(mod_full, 1)
            columns(0)

            def rest_of_setup(p):
                if p == 3:
                    dve.wait_ge(mod_full, 2)
                    columns(2)
                if p in (4, 8):
                    g = (p - 4) // 4
                    dve.wait_ge(mod_abs, g + 1)
                    sign = ge[1]
                    V.tensor_scalar(gbc[:, g, :], gbc[:, g, :], 0.25, None, ALU.max)
                    link0(V.tensor_scalar(sign[:], two(bp[1]), 0.0, 2.0, ALU.is_ge, ALU.mult))
                    V.scalar_tensor_tensor(two(gbc[:, g, :]), sign[:], -1.0, two(gbc[:, g, :]), ALU.add,
                                           ALU.mult).then_inc(mod_made, 1)
                if p == 18:
                    dve.wait_ge(fa_pe, 2)

            nlink = Links(dve, n_vlink, N_VLINKS)
            flink = Links(dve, f_vlink, F_VLINKS)
            rlink = Links(dve, r_vlink, R_VLINKS)

            def front(c, p):
                k = c.k
                if p == -5:
                    dve.wait_ge(x_in[c.par], 16 * c.turn + 16)
                    V.bn_stats(fst[:, 0, :], xt[c.par][:, 0, :])
                    nlink(c, V.bn_stats(fst[:, 1, :], xt[c.par][:, 1, :]), n=1)
                    V.memset(unused[:], 0.0)
                    V.bn_aggr(fmv[:, 0, :], fst[:, 0, :])
                    nlink(c, V.bn_aggr(fmv[:, 1, :], fst[:, 1, :]), n=2)
                    V.tensor_scalar(fmv[:, :, 1], fmv[:, :, 1], 1e-5, None, ALU.add).then_inc(f_var, 1)
                if p == -3:
                    dve.wait_ge(f_rstd, k + 1)
                    nlink(c, V.scalar_tensor_tensor(frs[:, :, 1], fmv[:, :, 0], -1.0, frs[:, :, 0], ALU.mult,
                                                    ALU.mult), n=3)
                    for tt in range(TT):
                        last = V.tensor_scalar(xt[c.par][:, tt, :], xt[c.par][:, tt, :], frs[:, tt, 0:1],
                                               frs[:, tt, 1:2], ALU.mult, ALU.add)
                    last.then_inc(f_xn, 1)
                if p in (9, 11, 13, 15):
                    i = (p - 9) // 2
                    s = slice(2 * i, 2 * i + 2)
                    dve.wait_ge(f_s, PAIRS * k + i + 1)
                    V.tensor_tensor(ub[:, s, :], ub[:, s, :], se[i % 2][:], ALU.mult).then_inc(f_u, 1)
                if 5 <= p < 5 + DB:
                    i, j = divmod(p - 5, 2)
                    m = 2 * i + j
                    if j == 0:
                        dve.wait_ge(f_used[i % 2], USES * k + 2 + i // 2)
                        if c.later(1):
                            dve.wait_ge(f_du, PAIRS * (k - 1) + i + 1)
                            dve.wait_ge(f_full[0], USES * (k - 1) + 6)
                        elif i == 0:
                            dve.wait_ge(w_loaded[0], w_all[0])
                        if i >= 2 or c.later(1):
                            dve.wait_ge(f_u, PAIRS * k + i - 1)
                    flink(c, V.tensor_scalar(ub[:, m, :], upre[:, m, 0:T], cw[:, m, 0:1], cb[:, m:m + 1],
                                             ALU.mult, ALU.add))
                    for q in range(1, K):
                        ins = V.scalar_tensor_tensor(ub[:, m, :], upre[:, m, q:q + T], cw[:, m, q:q + 1], ub[:, m, :],
                                                     ALU.mult, ALU.add)
                        if q < K - 1:
                            flink(c, ins)
                    ins.then_inc(f_tap, 1)
                    dve.wait_ge(f_tap, DB * k + m + 1)
                    V.tensor_copy(upre[:, m, 0:K - 1], upre[:, m, T:T + K - 1])
                    ins = V.tensor_scalar(se[i % 2][:, j, :], ub[:, m, :], LEAST, None, ALU.max)
                    if j:
                        ins.then_inc(f_conv, 1)
                if p == 17:
                    dve.wait_ge(f_full[0], USES * k + 5)
                    V.tensor_copy(ssm[:], fp[0][:, 0:TT * XP].rearrange("p (a b) -> p a b", a=TT)).then_inc(f_used[0], 1)
                    dve.wait_ge(f_used[0], USES * k + 5)
                    flink(c, V.tensor_tensor(ssq[:], ssm[:], ssm[:], ALU.mult))
                    V.reduce_sum(ms[:, :, 0], ssq[:, :, 0:R], AX)
                    flink(c, V.reduce_sum(ms[:, :, 1:3], ssq[:, :, R:].rearrange("p a (g b) -> p a g b", g=2), AX))
                    V.tensor_scalar(ms[:, :, 0], ms[:, :, 0], 1.0 / R, 1e-6, ALU.mult, ALU.add)
                    V.tensor_scalar(ms[:, :, 1:3], ms[:, :, 1:3], 1.0 / NS, 1e-6, ALU.mult, ALU.add).then_inc(f_ms, 1)
                if p == 19:
                    dve.wait_ge(f_mrstd, k + 1)
                    if c.later(1):
                        dve.wait_ge(f_full[1], USES * (k - 1) + 6)
                    if c.later(2):
                        dve.wait_ge(y_added, BANKS * (k - 1))
                    for tt in range(TT):
                        V.tensor_scalar(dtn[:, tt, :], ssm[:, tt, 0:R], mr[:, tt, 0:1], None, ALU.mult)
                        V.scalar_tensor_tensor(bn[:, tt, :], ssm[:, tt, R:R + NS], mr[:, tt, 1:2], bw[:],
                                               ALU.mult, ALU.mult)
                        last = V.scalar_tensor_tensor(cn[c.par][:, tt, :], ssm[:, tt, R + NS:], mr[:, tt, 2:3],
                                                      cwt[:], ALU.mult, ALU.mult)
                    last.then_inc(f_bc, 1)
                    flink.close(c)

            def add_states(k, par, n, h):
                item = ITEMS * k + 2 * n + h
                for tt in range(TT):
                    dve.wait_ge(st_turned, 2 * item + tt + 1)
                    if n:
                        dve.wait_ge(y_added, 2 * item + tt - 3)
                    else:
                        dve.wait_ge(f_used[tt], USES * k + 4 + (0 if h == 0 else 2 - tt))
                        dve.wait_ge(f_bc, k + 1)
                    o = acc[par][:, tt, h * 512:(h + 1) * 512]
                    V.scalar_tensor_tensor(o, stt[TT * h + tt][:, :], cn[par][:, tt, n:n + 1], o, ALU.mult,
                                           ALU.add).then_inc(y_added, 1)

            def scan(c, p):
                n, h = divmod(p, 2)
                item = ITEMS * c.k + p
                dve.wait_ge(drive_ready, item + 1)
                dve.wait_ge(decay_ready, item + 1)
                w = st[p % RING][:].rearrange("p a t -> p (a t)")
                V.tensor_tensor_scan(w, decay[h][:].rearrange("p a t -> p (a t)"), w, 0.0, ALU.mult,
                                     ALU.add).then_inc(scan_done, 1)
                if p >= ADD_LAG:
                    add_states(c.k, c.par, *divmod(p - ADD_LAG, 2))
                elif c.later(1):
                    add_states(c.k - 1, 1 - c.par, *divmod(p - ADD_LAG + ITEMS, 2))

            def back(c, p):
                k = c.k
                if 7 <= p < 7 + PAIRS:
                    i = p - 7
                    dve.wait_ge(r_full[i % 2], before(c, Y + i // 2) + 1)
                    dve.wait_ge(g_y, PAIRS * k + i + 1)
                    s = slice(2 * i, 2 * i + 2)
                    V.tensor_tensor(y[:, s, :], two(bp[i % 2]), y[:, s, :], ALU.mult).then_inc(r_used[i % 2], 1)
                if p in (15, 19):
                    tt = (p - 15) // 4
                    if tt == 0:
                        dve.wait_ge(xr_in, 16 * k + 16)
                    dve.wait_ge(r_full[tt], before(c, ATTN) + 1)
                    V.tensor_tensor(xr[:, tt, :], bp[tt][:, :], xr[:, tt, :], ALU.add).then_inc(r_used[tt], 1)
                    dve.wait_ge(r_used[tt], before(c, ATTN) + 1)
                    rlink(c, V.bn_stats(bst[:, tt, :], xr[:, tt, :]), tt == 1)
                    if tt:
                        V.memset(unused[:], 0.0)
                        for t2 in range(TT):
                            rlink(c, V.bn_aggr(bmv[:, t2, :], bst[:, t2, :]), t2 == TT - 1)
                        V.tensor_scalar(bmv[:, :, 1], bmv[:, :, 1], 1e-5, None, ALU.add).then_inc(r_var, 1)
                if p == 21:
                    dve.wait_ge(r_rstd, k + 1)
                    rlink(c, V.scalar_tensor_tensor(brs[:, :, 1], bmv[:, :, 0], -1.0, brs[:, :, 0], ALU.mult, ALU.mult))
                    for tt in range(TT):
                        last = V.tensor_scalar(x2[1 - c.par][:, tt, :], xr[:, tt, :], brs[:, tt, 0:1],
                                               brs[:, tt, 1:2], ALU.mult, ALU.add)
                    last.then_inc(r_xn, 1)
                if p in (32, 34):
                    tt = (p - 32) // 2
                    dve.wait_ge(r_full[tt], before(c, LIN) + 1)
                    V.tensor_tensor(xr[:, tt, :], bp[tt][:, :], xr[:, tt, :], ALU.add).then_inc(r_used[tt], 1)
                if p == ITEMS - 1:
                    rlink.close(c)

            def gates(c, p):
                if c.first():
                    rest_of_setup(p)
                if p in (19, 23, 28, 30):
                    i = (19, 23, 28, 30).index(p)
                    s = slice(2 * i, 2 * i + 2)
                    dve.wait_ge(r_used[i % 2], before_gates(c, i // 2) + 1)
                    if i >= 2 or c.later(1):
                        dve.wait_ge(g_y, PAIRS * c.k + i - 1)
                    V.tensor_scalar(ge[i % 2][:], y[:, s, :], LEAST, None, ALU.max).then_inc(g_cut, 1)
                if p in (22, 26, 31, 33):
                    i = (22, 26, 31, 33).index(p)
                    s = slice(2 * i, 2 * i + 2)
                    dve.wait_ge(g_s, PAIRS * c.k + i + 1)
                    V.tensor_tensor(y[:, s, :], y[:, s, :], ge[i % 2][:], ALU.mult).then_inc(g_y, 1)

            def scanned():
                for p in range(ITEMS - ADD_LAG, ITEMS):
                    add_states(NC - 1, 1, *divmod(p, 2))

            over_chunks(dve, front, scan, back, gates, scanned)

            t = [0]

            def tl(ins):
                t[0] += 1
                ins.then_inc(t_link, 1)
                dve.wait_ge(t_link, t[0])

            def each(v):
                return v[:, :, None].broadcast_to([P, lt, E])

            dve.wait_ge(t_act, 2)
            tl(V.reduce_max(tmx[:, 0:1], tw[0][:].rearrange("p a b -> p (a b)"), AX))
            tl(V.reduce_max(tmx[:, 1:2], tw[1][:].rearrange("p a b -> p (a b)"), AX))
            dve.wait_ge(t_red, 1)
            tl(V.tensor_scalar(tmr[:], tmr[:], 1e-6, 2.0, ALU.max, ALU.mult))
            tl(V.reciprocal(tmr[:], tmr[:]))
            tl(V.tensor_scalar(tw[2][:], ds[:], tmr[:, 1:2], None, ALU.mult))
            tl(V.scalar_tensor_tensor(tw[2][:], hs[:], tmr[:, 0:1], tw[2][:], ALU.mult, ALU.add))
            tl(V.reduce_max(tm[:, 0, :], tw[2][:], AX))
            tl(V.tensor_tensor(tw[2][:], tw[2][:], each(tm[:, 0, :]), ALU.subtract))
            dve.wait_ge(t_act, 3)
            tl(V.reduce_sum(tm[:, 1, :], tw[2][:], AX))
            tl(V.reciprocal(tm[:, 1, :], tm[:, 1, :]))
            tl(V.tensor_tensor(tw[2][:], tw[2][:], each(tm[:, 1, :]), ALU.mult))
            for i in range(lt):
                last = V.max(tw[4][:, i, :], tw[2][:, i, :])
            tl(last)
            tl(V.tensor_tensor(tw[3][:], tw[2][:], each(tw[4][:, :, 1]), ALU.subtract))
            dve.wait_ge(t_act, 5)
            tl(V.reciprocal(tw[3][:], tw[3][:]))
            tl(V.tensor_tensor(tw[2][:], tw[2][:], tw[3][:], ALU.mult))
            tl(V.reduce_sum(tm[:, 2, :], tw[2][:], AX))
            tl(V.tensor_scalar(tm[:, 2, :], tm[:, 2, :], 1e-9, None, ALU.add))
            tl(V.reciprocal(tm[:, 2, :], tm[:, 2, :]))
            tl(V.tensor_tensor(tw[0][:], tw[2][:], each(tm[:, 2, :]), ALU.mult))
            assert t[0] == TAIL_W, t[0]
            dve.wait_ge(z_in, 16)
            pbanks = [bp[0], bp[1], stt[0], stt[1]]
            for q in range(4):
                dve.wait_ge(t_pe, 4 + q + 1)
                z = zall[:, q * 512:(q + 1) * 512].rearrange("p (a b) -> p a b", b=2)
                pm = pbanks[q][0:RANK, :].rearrange("p (a b) -> p a b", b=2)[:, :, 1:2].broadcast_to([RANK, 256, 2])
                V.scalar_tensor_tensor(z, z, 0.5, pm, ALU.mult, ALU.mult).then_inc(t_link, 1)
            dve.wait_ge(base_in, 16 * len(base_tiles))
            banks = [fp[0], fp[1], stt[2], stt[3]]
            for i in range(lt):
                dve.wait_ge(t_pe, 8 + i + 1)
                o = base_tiles[i // 4][:, i % 4, :]
                V.tensor_tensor(o, banks[i % 4][:, :], o, ALU.add).then_inc(out_ready, 1)



INS = ["x", "w_in", "conv_w", "conv_b", "w_x", "dt_w", "b_w", "c_w", "w_dt", "dt_bias", "a_neg", "d_par", "w_out",
       "ffn_w", "ffn_b", "ffn_a", "bmat", "limes", "limes_t", "cond", "wmod"]


def kernel(**inputs):
    import numpy as np
    import concourse.bacc as bacc
    from concourse.bass_utils import run_bass_kernel_spmd as run

    v = {k: np.asarray(a) for k, a in inputs.items()}

    def tiles(a):
        return a.reshape(a.shape[0] // P, P, -1).transpose(1, 0, 2)

    def column(a):
        return a.reshape(-1, P).T

    at = "L0_attn_"
    data = {
        "x": v[at + "hidden_states"],
        "w_in": tiles(v[at + "W_in"].T),
        "conv_w": tiles(v[at + "conv_w"]),
        "conv_b": column(v[at + "conv_b"]),
        "w_x": tiles(v[at + "Wx"].T),
        "dt_w": v[at + "dt_ln_w"][:, None],
        "b_w": v[at + "b_ln_w"],
        "c_w": v[at + "c_ln_w"],
        "w_dt": v[at + "Wdt"].T,
        "dt_bias": column(v[at + "dt_bias"]),
        "a_neg": tiles(v[at + "A"]).transpose(0, 2, 1),
        "d_par": column(v[at + "D_param"]),
        "w_out": tiles(v[at + "W_out"].T),
        "ffn_w": tiles(v["L0_ffn_W"].T),
        "ffn_b": v["L0_ffn_b"][None, :],
        "ffn_a": tiles(v["L0_ffn_A"]),
        "bmat": v["L0_ffn_Bmat"],
        "limes": v["L0_ffn_LiMEs"],
        "limes_t": v["L0_ffn_LiMEs"].T,
        "cond": column(v["L0_c"][0]),
        "wmod": v["L0_wmod"],
    }
    nc = bacc.Bacc("TRN2", target_bir_lowering=False, num_devices=1)
    arrays, args = {}, []
    for name in INS:
        a = np.ascontiguousarray(data[name])
        arrays[name] = a
        args.append(nc.dram_tensor(name, a.shape, mybir.dt.from_np(a.dtype), kind="ExternalInput").ap())
    out = nc.dram_tensor("out", (1, L, H), mybir.dt.float32, kind="ExternalOutput").ap()
    build(nc, *args, out)
    r = run(nc, [arrays], core_ids=[0])
    return r.results[0]["out"]
```

```python
import concourse.bass as bass
from concourse import mybir
from contextlib import ExitStack

L, H, D, NS, R, K = 2048, 512, 1024, 16, 32, 4
E, RANK = 8, 32
P = 128
T = 256
NC = L // T
TT = T // P
DB = D // P
KT = H // P
HB = DB // 2
PAIRS = DB // 2
ITEMS = 2 * NS
BANKS = 2 * ITEMS
RING = 4
SAVE_LAG = 3
EARLY = 8
LATE = 7
ADD_LAG = 2
USES = 8
GROUP = 2
SLOT_LOADS = NS // GROUP // 2
XP = R + 2 * NS


class Chunk:

    def __init__(self, k, turn, par):
        self.k, self.turn, self.par = k, turn, par
        self.links = {}

    def first(self):
        return isinstance(self.k, int) and self.k == 0

    def later(self, n):
        return not isinstance(self.k, int) or self.k >= n


def static(k):
    return Chunk(k, k // 2, k % 2)


def build(nc, x, w_in, conv_w, conv_b, w_x, dt_w, b_w, c_w, w_dt, dt_bias, a_neg, d_par, w_out,
          ffn_w, ffn_b, ffn_a, bmat, limes, limes_t, cond, wmod, out):
    f32 = mybir.dt.float32
    ALU = mybir.AluOpType
    ACT = mybir.ActivationFunctionType
    AX = mybir.AxisListType.X
    with ExitStack() as ctx:
        def sb(name, *shape):
            return ctx.enter_context(nc.sbuf_tensor(name, list(shape), f32))

        def bank(name):
            return ctx.enter_context(nc.psum_tensor(name, [P, 512], f32))

        def sem(name):
            return ctx.enter_context(nc.semaphore(name))

        win = sb("win", P, KT, 2 * D)
        wx = sb("wx", P, DB, XP)
        wdt = sb("wdt", R, D)
        wout = sb("wout", P, DB, H)
        fw = sb("fw", P, KT, H)
        fw16 = sb("fw16", P, KT, 2 * E)
        fa = sb("fa", P, KT, RANK)
        fb = sb("fb", 1, H)
        fb16 = sb("fb16", 1, 2 * E)
        bm = sb("bm", RANK, H)
        lim = sb("lim", E, RANK)
        limt = sb("limt", RANK, E)
        an = sb("an", P, NS, DB)
        cw = sb("cw", P, DB, K)
        cb = sb("cb", P, DB)
        dtb = sb("dtb", P, DB)
        dp = sb("dp", P, DB)
        dtw = sb("dtw", R, 1)
        bw = sb("bw", P, NS)
        cwt = sb("cwt", P, NS)
        cnd = sb("cnd", P, KT)
        cnt = sb("cnt", P, 2, KT)
        mcol = sb("mcol", P, 4, KT)
        ident = sb("ident", P, P)
        ones = sb("ones", P, P)
        diag_d = sb("diag_d", P, DB, P)
        odd = sb("odd", P, 1)
        xt = [sb(f"xt{i}", P, TT, H) for i in range(2)]
        ht_in = [sb(f"ht_in{i}", P, KT, T) for i in range(2)]
        upre = sb("upre", P, DB, K - 1 + T)
        ub = sb("ub", P, DB, T)
        se = [sb(f"se{i}", P, 2, T) for i in range(2)]
        unused = sb("unused", P, 1)
        fst = sb("fst", P, TT, 6)
        fmv = sb("fmv", P, TT, 2)
        frs = sb("frs", P, TT, 2)
        ssm = sb("ssm", P, TT, XP)
        ssq = sb("ssq", P, TT, XP)
        ms = sb("ms", P, TT, 3)
        mr = sb("mr", P, TT, 3)
        dtn = sb("dtn", P, TT, R)
        bn = sb("bn", P, TT, NS)
        cn = [sb(f"cn{i}", P, TT, NS) for i in range(2)]
        dt_t = sb("dt_t", R, T)
        b_t = sb("b_t", NS, T)
        delta = [sb(f"delta{i}", P, DB, T) for i in range(2)]
        du = [sb(f"du{i}", P, DB, T) for i in range(2)]
        brow = [sb(f"brow{i}", P, GROUP, T) for i in range(2)]
        decay = [sb(f"decay{i}", P, HB, 1 + T) for i in range(2)]
        st = [sb(f"st{i}", P, HB, 1 + T) for i in range(RING)]
        carry = sb("carry", P, NS, DB)
        acc = [sb(f"acc{i}", P, TT, D) for i in range(2)]
        y = sb("y", P, DB, T)
        ge = [sb(f"ge{i}", P, 2, T) for i in range(2)]
        xr = sb("xr", P, TT, H)
        x2 = xt
        h2t = [t[:].rearrange("p a h -> p (a h)").rearrange("p (q t) -> p q t", q=KT) for t in xt]
        cbc = ge[0][:].rearrange("p a t -> p (a t)").rearrange("p (k m) -> p k m", k=KT)
        gbc = xr
        fa_t = ge[1][0:RANK, :, :].rearrange("p a t -> p (a t)")
        bst = sb("bst", P, TT, 6)
        bmv = sb("bmv", P, TT, 2)
        brs = sb("brs", P, TT, 2)
        zk = sb("zk", RANK, T)
        hd = sb("hd", P, L // P, 2 * E)
        hs, ds = hd[:, :, 0:E], hd[:, :, E:2 * E]
        lt = L // P
        tw = [st[0][:].rearrange("p a t -> p (a t)")[:, i * lt * E:(i + 1) * lt * E]
              .rearrange("p (a b) -> p a b", b=E) for i in range(5)]
        zall = y[0:RANK, :, :].rearrange("p a t -> p (a t)")
        tmx = sb("tmx", P, 2)
        tmr = sb("tmr", P, 2)
        tm = st[1][:].rearrange("p a t -> p (a t)")[:, 0:3 * lt].rearrange("p (a b) -> p a b", b=lt)

        b_dram = nc.dram_tensor("b_rows", [2, NS, T], f32, kind="Internal").ap()
        base_dram = nc.dram_tensor("base", [L, H], f32, kind="Internal").ap()

        z_dram = nc.dram_tensor("z", [NC * RANK, T], f32, kind="Internal").ap()

        stt = [bank(f"stt{i}") for i in range(2 * TT)]
        fp = [bank(f"fp{i}") for i in range(2)]
        bp = [bank(f"bp{i}") for i in range(2)]

        def nothing(c, p):
            pass

        def two(b):
            return (b if isinstance(b, bass.AP) else b[:, :]).rearrange("p (a t) -> p a t", a=2)

        w_loaded = [sem(f"w_loaded{i}") for i in range(4)]
        cond_loaded = sem("cond_loaded")
        mod_loaded = [sem(f"mod_loaded{i}") for i in range(3)]
        fa_pe = sem("fa_pe")
        fa_act = sem("fa_act")
        const_made = sem("const_made")
        cond_e = sem("cond_e")
        cond_u = sem("cond_u")
        cond_bc = sem("cond_bc")
        mod_full = sem("mod_full")
        mod_abs = sem("mod_abs")
        mod_made = sem("mod_made")
        folded = sem("folded")
        setup_link = sem("setup_link")
        setup_v = sem("setup_v")
        x_in = [sem(f"x_in{i}") for i in range(2)]
        f_full = [sem(f"f_full{i}") for i in range(2)]
        f_used = [sem(f"f_used{i}") for i in range(2)]
        f_var = sem("f_var")
        f_rstd = sem("f_rstd")
        f_xn = sem("f_xn")
        f_tap = sem("f_tap")
        f_conv = sem("f_conv")
        f_s = sem("f_s")
        f_u = sem("f_u")
        f_ms = sem("f_ms")
        f_mrstd = sem("f_mrstd")
        f_bc = sem("f_bc")
        f_ln = sem("f_ln")
        f_du = sem("f_du")
        n_vlink = sem("n_vlink")
        n_alink = sem("n_alink")
        f_vlink = sem("f_vlink")
        f_alink = sem("f_alink")
        f_glink = sem("f_glink")
        b_out = sem("b_out")
        brow_in = [sem(f"brow_in{i}") for i in range(2)]
        decay_ready = sem("decay_ready")
        scan_done = sem("scan_done")
        drive_ready = sem("drive_ready")
        carry_saved = sem("carry_saved")
        st_turned = sem("st_turned")
        y_added = sem("y_added")
        r_full = [sem(f"r_full{i}") for i in range(2)]
        r_used = [sem(f"r_used{i}") for i in range(2)]
        gated = [sem(f"gated{i}") for i in range(2)]
        g_cut = sem("g_cut")
        g_s = sem("g_s")
        g_alink = sem("g_alink")
        xr_in = sem("xr_in")
        r_var = sem("r_var")
        r_rstd = sem("r_rstd")
        r_xn = sem("r_xn")
        r_vlink = sem("r_vlink")
        r_alink = sem("r_alink")
        base_out = sem("base_out")
        z_free = sem("z_free")
        t_link = sem("t_link")
        t_act = sem("t_act")
        t_pe = sem("t_pe")
        t_red = sem("t_red")
        base_in = sem("base_in")
        z_in = sem("z_in")
        out_done = sem("out_done")

        GATE_USES = PAIRS // 2
        Y, ATTN, NORM, LIN, ADAPT = 0, 2, 3, 4, 5

        def before(c, use):
            last = isinstance(c.k, int) and c.k == NC - 1
            gates_between = 0 if last or use < NORM else 1 if use == NORM else 2
            return USES * c.k + GATE_USES + use + gates_between

        def before_gates(c, use):
            return use if c.first() else USES * c.k - 3 + 2 * use

        LEAST = -41.0
        N_VLINKS, N_ALINKS = 3, 1
        F_VLINKS, F_ALINKS, F_GLINKS = 18, 13, 4
        R_VLINKS, R_ALINKS, G_ALINKS = 5, 1, 2 * PAIRS

        class Links:

            def __init__(self, eng, s, per):
                self.eng, self.s, self.per = eng, s, per

            def __call__(self, c, ins, wait=True, n=None):
                if n is None:
                    n = c.links[self.s.name] = c.links.get(self.s.name, 0) + 1
                ins.then_inc(self.s, 1)
                if wait:
                    self.eng.wait_ge(self.s, self.per * c.k + n)

            def all_but(self, c, n):
                self.eng.wait_ge(self.s, self.per * c.k + c.links[self.s.name] - n)

            def close(self, c):
                assert c.links[self.s.name] == self.per, (self.s.name, c.links[self.s.name])

        out_ready = sem("out_ready")
        spots = [delta[0], du[0], delta[1], du[1], acc[1], y]
        base_tiles = [b[:].rearrange("p a b -> p (a b)").rearrange("p (t h) -> p t h", t=4)
                      for b in (delta[0], delta[1], du[0], du[1])]
        w_all = [16 * 10, 16, 16, 16 * 7]
        TAIL_W, TAIL_WT = 19, 5
        wt_all = [ub[0:E, 2 * q:2 * q + 2, :].rearrange("p a b -> p (a b)") for q in range(4)]

        def scan_inputs(ops, eng, link, c, p):
            for i, at in enumerate((27, 29, 31, 31)):
                if p == at:
                    s = slice(2 * i, 2 * i + 2)
                    eng.wait_ge(f_ln, PAIRS * c.k + i + 1)
                    link(c, ops.tensor_tensor(delta[c.par][:, s, :], delta[c.par][:, s, :], du[c.par][:, s, :],
                                              ALU.add))
                    ops.tensor_tensor(du[c.par][:, s, :], delta[c.par][:, s, :], ub[:, s, :],
                                      ALU.mult).then_inc(f_du, 1)

        block = ctx.enter_context(nc.Block())

        def over_chunks(eng, front, scan, back, gates, setup=lambda p: None, scanned=lambda: None):
            def chunk(prev2, prev, c, nxt, nxt2):
                for p in range(ITEMS):
                    scan(c, p)
                    late(prev2, prev, p)
                    if prev is not None:
                        back(prev, p)
                    if nxt is not None:
                        front(nxt, p)
                    if nxt2 is not None and p >= ITEMS - EARLY:
                        front(nxt2, p - ITEMS)
                    gates(c, p)

            def late(prev2, prev, p):
                if prev2 is not None and p < LATE:
                    back(prev2, ITEMS + p)
                if prev is not None and p < LATE:
                    gates(prev, ITEMS + p)

            c0 = static(0)
            for p in range(-EARLY, ITEMS):
                front(c0, p)
                setup(p)
                if p >= ITEMS - EARLY:
                    front(static(1), p - ITEMS)

            def at(k):
                return static(k) if 0 <= k < NC else None

            def fixed(k):
                chunk(at(k - 2), at(k - 1), at(k), at(k + 1), at(k + 2))

            fixed(0)
            fixed(1)
            with eng.Fori(0, NC // 2 - 2) as m:
                for j in range(2):
                    chunk(*(Chunk(2 * m + i, m + i // 2, i % 2) for i in range(j, j + 5)))
            fixed(NC - 2)
            fixed(NC - 1)
            scanned()
            last = static(NC - 1)
            for p in range(ITEMS):
                late(static(NC - 2), last, p)
                back(last, p)
            for p in range(LATE):
                back(last, ITEMS + p)

        @block.sync
        def _(sp):
            def load(dst, src, s):
                sp.dma_start(dst, src).then_inc(s, 16)

            def value(e):
                return e if isinstance(e, int) else sp.snap(e)

            load(cnd[:], cond, cond_loaded)
            mods = wmod.rearrange("(k p) (j n) -> j p k n", p=P, j=6)
            for j in (0, 1):
                load(spots[j][:].rearrange("p a b -> p (a b)").rearrange("p (k n) -> p k n", k=KT),
                     mods[j], mod_loaded[j])
            for i in range(2):
                load(xt[i][:], x[0, i * T:(i + 1) * T, :].rearrange("(t p) h -> p t h", p=P), x_in[i])
            load(bw[:], b_w[None, :].broadcast_to([P, NS]), w_loaded[0])
            load(cwt[:], c_w[None, :].broadcast_to([P, NS]), w_loaded[0])
            for dst, src in ((dtw, dt_w), (an, a_neg), (cw, conv_w), (cb, conv_b), (dtb, dt_bias),
                             (dp, d_par), (wx, w_x), (wdt, w_dt)):
                load(dst[:], src, w_loaded[0])
            load(win[:, :, 0:D], w_in[:, :, 0:D], w_loaded[1])
            for j in (2, 3, 4, 5):
                load(spots[j][:].rearrange("p a b -> p (a b)").rearrange("p (k n) -> p k n", k=KT),
                     mods[j], mod_loaded[2])
            load(win[:, :, D:2 * D], w_in[:, :, D:2 * D], w_loaded[2])
            for dst, src in ((wout, w_out), (fw, ffn_w), (fa, ffn_a), (fb, ffn_b), (bm, bmat),
                             (lim, limes), (limt, limes_t)):
                load(dst[:], src, w_loaded[3])

            def front(c, p):
                if p == -8 and c.later(2):
                    if c.later(3):
                        at, done = value(c.k * T), value(before(Chunk(c.k - 3, 0, 0), NORM) + 1)
                        sp.wait_ge(r_full[1], done)
                    else:
                        at = c.k * T
                        sp.wait_ge(f_full[1], 1)
                    load(xt[c.par][:], x[0, bass.ds(at, T), :].rearrange("(t p) h -> p t h", p=P),
                         x_in[c.par])
                if p == 24:
                    sp.wait_ge(f_used[1], USES * c.k + 6)
                    load(b_dram[c.par], b_t[:], b_out)

            def scan(c, p):
                if p == 0:
                    rows(c, 0)
                    rows(c, 1)
                elif p % (2 * GROUP) == 0 and p + 2 * GROUP < ITEMS:
                    rows(c, p // (2 * GROUP) + 1)

            def rows(c, g):
                if g == 0:
                    sp.wait_ge(b_out, 16 * c.k + 16)
                if g >= 2 or c.later(1):
                    sp.wait_ge(drive_ready, ITEMS * c.k + 2 * GROUP * (g - 1))
                load(brow[g % 2][:], b_dram[c.par, GROUP * g:GROUP * (g + 1), :][None].broadcast_to([P, GROUP, T]),
                     brow_in[g % 2])

            def back(c, p):
                if p == 7:
                    at = value(c.k * T)
                    if c.later(1):
                        sp.wait_ge(base_out, 32 * c.k)
                    else:
                        sp.wait_ge(folded, 3)
                    load(xr[:], x[0, bass.ds(at, T), :].rearrange("(t p) h -> p t h", p=P), xr_in)
                if p in (ITEMS + 1, ITEMS + 3):
                    tt = (p - ITEMS - 1) // 2
                    at, done = value(c.k * T + tt * P), value(before(c, LIN) + 1)
                    sp.wait_ge(r_used[tt], done)
                    load(base_dram[bass.ds(at, P), :], xr[:, tt, :], base_out)
                if p == ITEMS + 6:
                    at, done = value(c.k * RANK), value(before(c, ADAPT) + 1)
                    sp.wait_ge(r_used[1], done)
                    load(z_dram[bass.ds(at, RANK), :], zk[:], z_free)

            over_chunks(sp, front, scan, back, nothing)
            sp.wait_ge(z_free, 16 * NC + 16)
            sp.wait_ge(r_full[0], USES * NC)
            load(zall.rearrange("r (c t) -> r c t", c=NC), z_dram.rearrange("(c r) t -> r c t", c=NC), z_in)
            sp.wait_ge(base_out, 32 * NC)
            sp.wait_ge(y_added, BANKS * NC)
            for q, b in enumerate(base_tiles):
                load(b, base_dram[q * 512:(q + 1) * 512, :].rearrange("(t p) h -> p t h", p=P), base_in)
            for q, b in enumerate(base_tiles):
                sp.wait_ge(out_ready, 4 * (q + 1))
                load(out[0, q * 512:(q + 1) * 512, :].rearrange("(t p) h -> p t h", p=P), b, out_done)
            sp.wait_ge(out_done, 16 * len(base_tiles))


        @block.tensor
        def _(pe):
            def mm(o, a, b, start=True, stop=True):
                return nc.tensor.matmul(o, a, b, start=start, stop=stop)

            wm = [s[:].rearrange("p a b -> p (a b)").rearrange("p (k n) -> p k n", k=KT) for s in spots]

            def mod_columns(pieces):
                for g, j in enumerate(pieces):
                    if j < 2:
                        pe.wait_ge(mod_loaded[j], 16)
                    for m in range(KT):
                        for q in range(KT):
                            last = mm(bp[0][:, g * KT + m:g * KT + m + 1], wm[j][:, q, m * P:(m + 1) * P],
                                      cnt[:, 1, q:q + 1], q == 0, q == KT - 1)
                last.then_inc(mod_full, 1)

            def mod_rows(j):
                for q in range(KT):
                    last = mm(bp[1][:, :], cbc[:, q, :], wm[j][:, q, :], q == 0, q == KT - 1)
                last.then_inc(mod_full, 1)

            pe.wait_ge(cond_u, 1)
            mod_columns((0, 1))
            pe.wait_ge(const_made, 3)

            def setup(p):
                if p == 10:
                    pe.wait_ge(mod_loaded[2], 16 * 4)
                    mod_columns((3, 4))
                if p == 16:
                    pe.wait_ge(cond_bc, 1)
                    mod_rows(2)
                if p == 19:
                    pe.wait_ge(mod_made, 5)
                    mod_rows(5)
                if p == 23:
                    pe.wait_ge(w_loaded[3], w_all[3])
                    for q in range(KT):
                        last = nc.tensor.transpose(bp[0][0:RANK, q * P:(q + 1) * P], fa[:, q, :], ident[:])
                    last.then_inc(fa_pe, 1)
                if p == 27:
                    pe.wait_ge(fa_act, 1)
                    for q in range(KT):
                        last = mm(bp[0][:, q * E:(q + 1) * E], fa_t[:, q * P:(q + 1) * P], limt[:])
                    last.then_inc(fa_pe, 1)

            def free(c, b, u):
                if u or c.later(1):
                    pe.wait_ge(f_used[b], USES * c.k + u)

            def rfree(b, uses):
                if not isinstance(uses, int) or uses:
                    pe.wait_ge(r_used[b], uses)

            def start_sum(c, h, tt, u):
                free(c, tt, u)
                for j in range(HB):
                    last = mm(fp[tt][:, j * P:(j + 1) * P], ub[:, HB * h + j, tt * P:(tt + 1) * P],
                              diag_d[:, HB * h + j, :])
                last.then_inc(f_full[tt], 1)

            def front(c, p):
                if p == -2:
                    pe.wait_ge(f_xn, c.k + 1)
                    for b in range(2):
                        free(c, b, 0)
                        for j in range(2):
                            for tt in range(TT):
                                last = nc.tensor.transpose(
                                    two(fp[b])[:, j, tt * P:(tt + 1) * P],
                                    xt[c.par][:, tt, (2 * b + j) * P:(2 * b + j + 1) * P], ident[:])
                        last.then_inc(f_full[b], 1)
                if 2 <= p < 2 + DB:
                    i, j = divmod(p - 2, 2)
                    if p == 2:
                        pe.wait_ge(f_used[0], USES * c.k + 1)
                        pe.wait_ge(f_used[1], USES * c.k + 1)
                        if c.first():
                            pe.wait_ge(w_loaded[1], 16)
                    if j == 0:
                        free(c, i % 2, 1 + i // 2)
                    for q in range(KT):
                        last = mm(two(fp[i % 2])[:, j, :], win[:, q, (2 * i + j) * P:(2 * i + j + 1) * P],
                                  ht_in[c.par][:, q, :], q == 0, q == KT - 1)
                    if j:
                        last.then_inc(f_full[i % 2], 1)
                if p == 12:
                    pe.wait_ge(f_u, PAIRS * c.k + 2)
                    if c.first():
                        pe.wait_ge(folded, 1)
                    start_sum(c, 0, 0, 3)
                    start_sum(c, 0, 1, 3)
                if p == 15:
                    pe.wait_ge(f_u, PAIRS * c.k + PAIRS)
                    free(c, 0, 4)
                    for tt in range(TT):
                        for i in range(DB):
                            last = mm(fp[0][:, tt * XP:(tt + 1) * XP], ub[:, i, tt * P:(tt + 1) * P], wx[:, i, :],
                                      i == 0, i == DB - 1)
                    last.then_inc(f_full[0], 1)
                if p == 17:
                    start_sum(c, 1, 1, 4)
                if p == 18:
                    start_sum(c, 1, 0, 5)
                if p == 21:
                    pe.wait_ge(f_bc, c.k + 1)
                    free(c, 1, 5)
                    for tt in range(TT):
                        nc.tensor.transpose(fp[1][0:R, tt * P:(tt + 1) * P], dtn[:, tt, :], ident[:])
                        last = nc.tensor.transpose(fp[1][0:NS, T + tt * P:T + (tt + 1) * P], bn[:, tt, :], ident[:])
                    last.then_inc(f_full[1], 1)
                if p in (22, 23, 25, 27):
                    i = (22, 23, 25, 27).index(p)
                    b = i % 2
                    if i == 0:
                        pe.wait_ge(f_used[1], USES * c.k + 6)
                    free(c, b, 6 + i // 2)
                    for j in range(2):
                        last = mm(two(fp[b])[:, j, :], wdt[:, (2 * i + j) * P:(2 * i + j + 1) * P], dt_t[:])
                    last.then_inc(f_full[b], 1)

            def scan(c, p):
                item, h = ITEMS * c.k + p, p % 2
                pe.wait_ge(scan_done, item + 1)
                for tt in range(TT):
                    if p >= 2 or c.later(1):
                        pe.wait_ge(y_added, 2 * item + tt - 3)
                    for j in range(HB):
                        last = nc.tensor.transpose(stt[TT * h + tt][:, j * P:(j + 1) * P],
                                                   st[p % RING][:, j, 1 + tt * P:1 + (tt + 1) * P], ident[:])
                    last.then_inc(st_turned, 1)

            def back(c, p):
                if 5 <= p < 5 + PAIRS:
                    i = p - 5
                    if i == 0:
                        pe.wait_ge(y_added, BANKS * c.k + BANKS)
                    rfree(i % 2, before(c, Y + i // 2))
                    for j in range(2):
                        for tt in range(TT):
                            last = nc.tensor.transpose(
                                two(bp[i % 2])[:, j, tt * P:(tt + 1) * P],
                                acc[c.par][:, tt, (2 * i + j) * P:(2 * i + j + 1) * P], ident[:])
                    last.then_inc(r_full[i % 2], 1)
                if 10 <= p < 18:
                    if p == 10:
                        rfree(0, before(c, ATTN))
                        rfree(1, before(c, ATTN))
                        if c.first():
                            pe.wait_ge(folded, 3)
                    tt, part = divmod(p - 10, 4)
                    for i in (2 * part, 2 * part + 1):
                        last = mm(bp[tt][:, :], y[:, i, tt * P:(tt + 1) * P], wout[:, i, :], i == 0, i == DB - 1)
                    if part == 3:
                        last.then_inc(r_full[tt], 1)
                if p == 23:
                    pe.wait_ge(r_xn, c.k + 1)
                    for b in range(2):
                        rfree(b, before(c, NORM))
                        for j in range(2):
                            for tt in range(TT):
                                last = nc.tensor.transpose(
                                    two(bp[b])[:, j, tt * P:(tt + 1) * P],
                                    x2[1 - c.par][:, tt, (2 * b + j) * P:(2 * b + j + 1) * P], ident[:])
                        last.then_inc(r_full[b], 1)
                if 29 <= p < 33:
                    tt, part = divmod(p - 29, 2)
                    if part == 0:
                        rfree(tt, before(c, LIN))
                        rfree(1, before(c, NORM) + 1)
                    for q in (2 * part, 2 * part + 1):
                        mm(bp[tt][:, :], h2t[c.par][:, q, tt * P:(tt + 1) * P], fw[:, q, :], q == 0, False)
                    if part:
                        mm(bp[tt][:, :], ones[0:1, :], fb[:], False, True).then_inc(r_full[tt], 1)
                if p == 33:
                    rfree(0, before(c, ADAPT))
                    if c.first():
                        pe.wait_ge(folded, 2)
                    w = 2 * E
                    for tt in range(TT):
                        for q in range(KT):
                            mm(bp[0][:, tt * w:(tt + 1) * w], h2t[c.par][:, q, tt * P:(tt + 1) * P],
                               fw16[:, q, :], q == 0, False)
                        last = mm(bp[0][:, tt * w:(tt + 1) * w], ones[0:1, :], fb16[:], False, True)
                    last.then_inc(r_full[0], 1)
                if p == 35:
                    rfree(1, before(c, ADAPT))
                    for q in range(KT):
                        last = mm(bp[1][0:RANK, 0:T], fa[:, q, :], h2t[c.par][:, q, :], q == 0, q == KT - 1)
                    last.then_inc(r_full[1], 1)

            def gates(c, p):
                if c.first() and p == 18:
                    pe.wait_ge(fa_act, 2)
                    pe.wait_ge(mod_made, 6)
                if p in (18, 19, 20, 21, 25, 26, 28, 29):
                    i, j = divmod((18, 19, 20, 21, 25, 26, 28, 29).index(p), 2)
                    if c.first() and p == 18:
                        pe.wait_ge(w_loaded[2], 16)
                    if j == 0:
                        rfree(i % 2, before_gates(c, i // 2))
                    for q in range(KT):
                        last = mm(two(bp[i % 2])[:, j, :], win[:, q, D + (2 * i + j) * P:D + (2 * i + j + 1) * P],
                                  ht_in[c.par][:, q, :], q == 0, q == KT - 1)
                    if j:
                        last.then_inc(r_full[i % 2], 1)

            over_chunks(pe, front, scan, back, gates, setup)
            pe.wait_ge(t_link, TAIL_W)
            pe.wait_ge(f_used[0], USES * NC)
            pe.wait_ge(f_used[1], USES * NC)
            banks = [fp[0], fp[1], stt[2], stt[3]]
            for q in range(4):
                for i in range(4):
                    last = nc.tensor.transpose(banks[q][0:E, i * P:(i + 1) * P], tw[0][:, 4 * q + i, :], ident[:])
                last.then_inc(t_pe, 1)
            pbanks = [bp[0], bp[1], stt[0], stt[1]]
            rfree(0, USES * NC)
            rfree(1, USES * NC)
            for q in range(4):
                pe.wait_ge(t_act, TAIL_WT + q + 1)
                mm(pbanks[q][0:RANK, 0:256], lim[:], wt_all[q].rearrange("p (a b) -> p b a", b=2)[:, 1, :]).then_inc(t_pe, 1)
            for i in range(L // P):
                if i % 4 == 0:
                    pe.wait_ge(t_link, TAIL_W + i // 4 + 1)
                if i >= 4:
                    pe.wait_ge(out_ready, i - 3)
                mm(banks[i % 4][:, :], zall[:, i * P:(i + 1) * P], bm[:]).then_inc(t_pe, 1)


        @block.scalar
        def _(act):
            A = nc.scalar.activation
            nc.scalar.preload_act_table_set("natural_log_exp_and_others")
            act.wait_ge(cond_loaded, 16)
            A(cnt[:, 0, :], cnd[:], ACT.Exp, scale=-1.0).then_inc(cond_e, 1)

            def setup(p):
                if p == 0:
                    act.wait_ge(mod_made, 2)
                    act.wait_ge(w_loaded[0], w_all[0])
                if p in (17, 20):
                    g = (p - 17) // 3
                    act.wait_ge(mod_full, 3 + g)
                    A(gbc[:, g, :], bp[1][:, :], ACT.Abs).then_inc(mod_abs, 1)
                if p == 25:
                    act.wait_ge(fa_pe, 1)
                    act.wait_ge(mod_made, 6)
                    A(fa_t, bp[0][0:RANK, :], ACT.Copy).then_inc(fa_act, 1)
                if p == 30:
                    act.wait_ge(fa_pe, 2)
                    A(fw16[:, :, E:2 * E], bp[0][:, 0:KT * E].rearrange("p (a b) -> p a b", a=KT),
                      ACT.Copy).then_inc(fa_act, 1)

            nlink = Links(act, n_alink, N_ALINKS)
            flink = Links(act, f_alink, F_ALINKS)
            rlink = Links(act, r_alink, R_ALINKS)
            glink = Links(act, g_alink, G_ALINKS)

            def front(c, p):
                k = c.k
                if p == -3:
                    act.wait_ge(f_var, k + 1)
                    nlink(c, A(frs[:, :, 0], fmv[:, :, 1], ACT.Ln), n=1)
                    A(frs[:, :, 0], frs[:, :, 0], ACT.Exp, scale=-0.5).then_inc(f_rstd, 1)
                if p in (1, 2):
                    b = p - 1
                    if c.later(2) and b == 0:
                        act.wait_ge(r_full[1], before_gates(static(k - 2) if isinstance(k, int) else
                                                            Chunk(k - 2, 0, 0), 1) + 1)
                    act.wait_ge(f_full[b], USES * k + 1)
                    for j in range(2):
                        q = 2 * b + j
                        last = A(ht_in[c.par][:, q, :], two(fp[b])[:, j, :], ACT.Identity,
                                 scale=mcol[:, 1, q:q + 1], bias=mcol[:, 0, q:q + 1])
                    last.then_inc(f_used[b], 1)
                if p in (5, 7, 9, 11):
                    i = (p - 5) // 2
                    act.wait_ge(f_full[i % 2], USES * k + 2 + i // 2)
                    if c.later(1):
                        act.wait_ge(f_conv, PAIRS * (k - 1) + i + 1)
                        act.wait_ge(f_du, PAIRS * (k - 1) + i + 1)
                        act.wait_ge(f_full[0], USES * (k - 1) + 6)
                    else:
                        act.wait_ge(const_made, 3)
                    A(upre[:, 2 * i:2 * i + 2, K - 1:], two(fp[i % 2]), ACT.Copy)
                    for j in range(2):
                        m = 2 * i + j
                        last = A(ub[:, m, :], two(fp[i % 2])[:, j, :], ACT.Identity, scale=cw[:, m, K - 1:K],
                                 bias=cb[:, m:m + 1])
                    last.then_inc(f_used[i % 2], 1)
                if p in (8, 10, 12, 14):
                    i = (p - 8) // 2
                    act.wait_ge(f_conv, PAIRS * k + i + 1)
                    flink(c, A(se[i % 2][:], se[i % 2][:], ACT.Exp, scale=-1.0))
                    flink(c, A(se[i % 2][:], se[i % 2][:], ACT.Ln, bias=1.0))
                    A(se[i % 2][:], se[i % 2][:], ACT.Exp, scale=-1.0).then_inc(f_s, 1)
                for at, h, tt, use in ((15, 0, 0, 3), (15, 0, 1, 3), (20, 1, 1, 4), (21, 1, 0, 5)):
                    if p == at:
                        act.wait_ge(f_full[tt], USES * k + use + 1)
                        A(acc[c.par][:, tt, h * 512:(h + 1) * 512], fp[tt][:, :], ACT.Copy).then_inc(f_used[tt], 1)
                if p == 19:
                    act.wait_ge(f_ms, k + 1)
                    flink(c, A(mr[:], ms[:], ACT.Ln))
                    A(mr[:], mr[:], ACT.Exp, scale=-0.5).then_inc(f_mrstd, 1)
                if p == 23:
                    act.wait_ge(f_full[1], USES * k + 6)
                    if c.later(1):
                        act.wait_ge(f_full[1], USES * k)
                        act.wait_ge(b_out, 16 * k)
                    A(dt_t[:], fp[1][0:R, 0:T], ACT.Copy)
                    A(b_t[:], fp[1][0:NS, T:2 * T], ACT.Copy).then_inc(f_used[1], 1)
                dl, e = delta[c.par], du[c.par]
                if p in (25, 27, 29, 30):
                    i = (25, 27, 29, 30).index(p)
                    act.wait_ge(f_used[i % 2], USES * k + 7 + i // 2)
                    s = slice(2 * i, 2 * i + 2)
                    flink(c, A(e[:, s, :], e[:, s, :], ACT.Exp, scale=-1.0))
                    A(e[:, s, :], e[:, s, :], ACT.Ln, bias=1.0).then_inc(f_ln, 1)
                if p in (24, 26, 28, 29):
                    i = (24, 26, 28, 29).index(p)
                    b = i % 2
                    act.wait_ge(f_full[b], USES * k + 7 + i // 2)
                    if c.later(2):
                        act.wait_ge(decay_ready, ITEMS * (k - 1))
                        act.wait_ge(drive_ready, ITEMS * (k - 1))
                    for j in range(2):
                        m = 2 * i + j
                        A(e[:, m, :], two(fp[b])[:, j, :], ACT.Abs, bias=dtb[:, m:m + 1])
                        last = A(dl[:, m, :], two(fp[b])[:, j, :], ACT.Relu, bias=dtb[:, m:m + 1])
                    last.then_inc(f_used[b], 1)
                if p == ITEMS - 1:
                    flink.close(c)

            def scan(c, p):
                n, h = divmod(p, 2)
                if c.first() and n == 0:
                    act.wait_ge(const_made, 3)
                if n == 0:
                    act.wait_ge(f_du, PAIRS * c.k + 2 * h + 2)
                if p >= 2 or c.later(1):
                    act.wait_ge(scan_done, ITEMS * c.k + p - 1)
                for j in range(HB):
                    m = HB * h + j
                    last = A(decay[h][:, j, 1:], delta[c.par][:, m, :], ACT.Exp, scale=an[:, n, m:m + 1])
                last.then_inc(decay_ready, 1)

            def back(c, p):
                k = c.k
                if p == 21:
                    act.wait_ge(r_var, k + 1)
                    rlink(c, A(brs[:, :, 0], bmv[:, :, 1], ACT.Ln))
                    A(brs[:, :, 0], brs[:, :, 0], ACT.Exp, scale=-0.5).then_inc(r_rstd, 1)
                if p in (25, 27):
                    b = (p - 25) // 2
                    act.wait_ge(r_full[b], before(c, NORM) + 1)
                    for j in range(2):
                        q = 2 * b + j
                        last = A(h2t[c.par][:, q, :], two(bp[b])[:, j, :], ACT.Identity,
                                 scale=mcol[:, 3, q:q + 1], bias=mcol[:, 2, q:q + 1])
                    last.then_inc(r_used[b], 1)
                if p == 36:
                    act.wait_ge(r_full[0], before(c, ADAPT) + 1)
                    A(hd[:, bass.ds(TT * k, TT), :], bp[0][:, 0:TT * 2 * E].rearrange("p (a b) -> p a b", a=TT),
                      ACT.Copy).then_inc(r_used[0], 1)
                if p == 37:
                    act.wait_ge(z_free, 16 * k + 16)
                    act.wait_ge(r_full[1], before(c, ADAPT) + 1)
                    A(zk[:], bp[1][0:RANK, 0:T], ACT.Copy).then_inc(r_used[1], 1)
                if p == ITEMS - 1:
                    rlink.close(c)

            def gates(c, p):
                k = c.k
                if p in (21, 23, 28, 31):
                    i = (21, 23, 28, 31).index(p)
                    s = slice(2 * i, 2 * i + 2)
                    act.wait_ge(r_full[i % 2], before_gates(c, i // 2) + 1)
                    A(y[:, s, :], two(bp[i % 2]), ACT.Copy).then_inc(r_used[i % 2], 1)
                if p in (23, 31, 32, 35):
                    i = (23, 31, 32, 35).index(p)
                    act.wait_ge(g_cut, PAIRS * k + i + 1)
                    glink(c, A(ge[i % 2][:], ge[i % 2][:], ACT.Exp, scale=-1.0), n=2 * i + 1)
                    glink(c, A(ge[i % 2][:], ge[i % 2][:], ACT.Ln, bias=1.0), n=2 * i + 2)
                    A(ge[i % 2][:], ge[i % 2][:], ACT.Exp, scale=-1.0).then_inc(g_s, 1)

            over_chunks(act, front, scan, back, gates, setup)
            act.wait_ge(r_used[0], USES * NC)
            act.wait_ge(r_used[1], USES * NC)
            A(tw[0][:], hs[:], ACT.Abs, scale=odd[:]).then_inc(t_act, 1)
            A(tw[1][:], ds[:], ACT.Abs, scale=odd[:]).then_inc(t_act, 1)
            act.wait_ge(t_link, 8)
            A(tw[2][:], tw[2][:], ACT.Exp).then_inc(t_act, 1)
            act.wait_ge(t_link, 13)
            A(tw[3][:], tw[3][:], ACT.Exp, scale=-2.0).then_inc(t_act, 1)
            act.wait_ge(t_act, 4)
            A(tw[3][:], tw[3][:], ACT.Identity, bias=1.0).then_inc(t_act, 1)
            banks = [fp[0], fp[1], stt[2], stt[3]]
            for q in range(4):
                act.wait_ge(t_pe, q + 1)
                A(wt_all[q], banks[q][0:E, :], ACT.Copy).then_inc(t_act, 1)

        @block.gpsimd
        def _(gp):
            G = nc.gpsimd
            G.memset(ident[:], 0.0).then_inc(setup_link, 1)
            G.memset(ones[:], 1.0).then_inc(const_made, 1)
            gp.wait_ge(setup_link, 1)
            G.affine_select(out=ident[:], in_=ident[:], compare_op=ALU.not_equal, fill=1.0, base=0,
                            pattern=[[-1, P]], channel_multiplier=1).then_inc(const_made, 1)
            G.memset(upre[:, :, 0:K - 1], 0.0)
            for b in decay:
                G.memset(b[:, :, 0:1], 0.0)
            G.memset(fb16[:], 0.0)
            G.memset(zk[:], 0.0).then_inc(z_free, 16)
            G.memset(carry[:], 0.0).then_inc(const_made, 1)
            gp.wait_ge(const_made, 3)
            gp.wait_ge(w_loaded[0], w_all[0])
            for i in range(DB):
                G.tensor_scalar(diag_d[:, i, :], ident[:], dp[:, i:i + 1], 1.0, ALU.mult, ALU.mult)
            G.tensor_scalar(wdt[:], wdt[:], dtw[:], 1.0, ALU.mult, ALU.mult).then_inc(folded, 1)
            glink = Links(gp, f_glink, F_GLINKS)

            def setup(p):
                if p == 16:
                    gp.wait_ge(w_loaded[3], w_all[3])
                    G.tensor_copy(fw16[:, :, 0:E], fw[:, :, 0:E])
                    G.tensor_copy(fb16[:, 0:E], fb[:, 0:E]).then_inc(folded, 1)
                if p == 18:
                    gp.wait_ge(mod_made, 5)
                    G.tensor_tensor(wout[:], wout[:], gbc[:, 0:1, :].broadcast_to([P, DB, H]), ALU.mult)

            def fold(p):
                if 16 <= p < 16 + KT:
                    q = p - 16
                    if q == 0:
                        gp.wait_ge(mod_made, 6)
                        gp.wait_ge(folded, 2)
                    G.tensor_tensor(fw[:, q, :], fw[:, q, :], gbc[:, 1, :], ALU.mult)
                if p == 16 + KT:
                    G.tensor_tensor(fb[:], fb[:], gbc[0:1, 1, :], ALU.mult)
                    G.tensor_tensor(bm[:], bm[:], gbc[0:RANK, 1, :], ALU.mult).then_inc(folded, 1)

            def front(c, p):
                if p in (9, 11, 13, 15):
                    i = (p - 9) // 2
                    s = slice(2 * i, 2 * i + 2)
                    gp.wait_ge(f_s, PAIRS * c.k + i + 1)
                    G.tensor_tensor(ub[:, s, :], ub[:, s, :], se[i % 2][:], ALU.mult).then_inc(f_u, 1)
                if not c.first():
                    scan_inputs(G, gp, glink, c, p)
                if p == ITEMS - 1 and not c.first():
                    glink.close(c)

            def scan(c, p):
                n, h = divmod(p, 2)
                item = ITEMS * c.k + p
                if n % GROUP == 0 and h == 0:
                    g = n // GROUP
                    gp.wait_ge(brow_in[g % 2], 16 * SLOT_LOADS * c.k + 16 * (g // 2) + 16)
                if n == 0:
                    gp.wait_ge(f_du, PAIRS * c.k + 2 * h + 2)
                w = st[p % RING]
                if p >= RING or c.later(1):
                    gp.wait_ge(st_turned, 2 * item - 6)
                    gp.wait_ge(carry_saved, item - 3)
                if p >= SAVE_LAG or c.later(1):
                    gp.wait_ge(scan_done, item - SAVE_LAG + 1)
                G.tensor_tensor(w[:, :, 1:], du[c.par][:, HB * h:HB * (h + 1), :],
                                brow[(n // GROUP) % 2][:, n % GROUP:n % GROUP + 1, :].broadcast_to([P, HB, T]),
                                ALU.mult)
                G.tensor_copy(w[:, :, 0], carry[:, n, HB * h:HB * (h + 1)]).then_inc(drive_ready, 1)
                if p >= SAVE_LAG or c.later(1):
                    m, g = divmod((p - SAVE_LAG) % ITEMS, 2)
                    G.tensor_copy(carry[:, m, HB * g:HB * (g + 1)],
                                  st[(p - SAVE_LAG) % RING][:, :, T]).then_inc(carry_saved, 1)
                if c.first():
                    fold(p)

            def gates(c, p):
                if p in (ITEMS + 5, ITEMS + 6):
                    i = p - ITEMS - 3
                    s = slice(2 * i, 2 * i + 2)
                    gp.wait_ge(g_s, PAIRS * c.k + i + 1)
                    G.tensor_tensor(y[:, s, :], y[:, s, :], ge[i % 2][:], ALU.mult).then_inc(gated[1], 1)

            over_chunks(gp, front, scan, nothing, gates, setup)
            gp.wait_ge(t_link, 2)
            G.partition_all_reduce(tmr[:], tmx[:], P, bass.bass_isa.ReduceOp.max).then_inc(t_red, 1)

        @block.vector
        def _(dve):
            V = nc.vector
            steps = [0]

            def link0(ins):
                steps[0] += 1
                ins.then_inc(setup_v, 1)
                dve.wait_ge(setup_v, steps[0])

            dve.wait_ge(const_made, 3)
            link0(V.reduce_sum(odd[:], ident[:].rearrange("p (a b) -> p b a", b=2)[:, 1, :], AX))
            dve.wait_ge(cond_e, 1)
            link0(V.tensor_scalar(cnt[:, 0, :], cnt[:, 0, :], 1.0, None, ALU.add))
            link0(V.reciprocal(cnt[:, 0, :], cnt[:, 0, :]))
            V.tensor_tensor(cnt[:, 1, :], cnt[:, 0, :], cnd[:], ALU.mult).then_inc(cond_u, 1)
            dve.wait_ge(cond_u, 1)
            for q in range(KT):
                last = V.tensor_scalar(cbc[:, q, :], ones[:], cnt[:, 1, q:q + 1], None, ALU.mult)
            last.then_inc(cond_bc, 1)

            def columns(g):
                mv = bp[0][:, 0:2 * KT].rearrange("p (g m) -> p g m", g=2)
                V.tensor_copy(mcol[:, g:g + 2, :], mv).then_inc(mod_made, 1)
                dve.wait_ge(mod_made, 1 if g == 0 else 3)
                V.tensor_scalar(mcol[:, g + 1, :], mcol[:, g + 1, :], 1.0, None, ALU.add).then_inc(mod_made, 1)

            def setup(p):
                if p == -2:
                    dve.wait_ge(mod_full, 1)
                    columns(0)
                if p == 14:
                    dve.wait_ge(mod_full, 2)
                    columns(2)
                if p in (18, 21):
                    g = (p - 18) // 3
                    dve.wait_ge(mod_abs, g + 1)
                    sign = ge[1]
                    V.tensor_scalar(gbc[:, g, :], gbc[:, g, :], 0.25, None, ALU.max)
                    link0(V.tensor_scalar(sign[:], two(bp[1]), 0.0, 2.0, ALU.is_ge, ALU.mult))
                    V.scalar_tensor_tensor(two(gbc[:, g, :]), sign[:], -1.0, two(gbc[:, g, :]), ALU.add,
                                           ALU.mult).then_inc(mod_made, 1)

            nlink = Links(dve, n_vlink, N_VLINKS)
            flink = Links(dve, f_vlink, F_VLINKS)
            dlink = Links(dve, f_glink, F_GLINKS)
            rlink = Links(dve, r_vlink, R_VLINKS)

            def front(c, p):
                k = c.k
                if p == -5:
                    dve.wait_ge(x_in[c.par], 16 * c.turn + 16)
                    V.bn_stats(fst[:, 0, :], xt[c.par][:, 0, :])
                    nlink(c, V.bn_stats(fst[:, 1, :], xt[c.par][:, 1, :]), n=1)
                    V.memset(unused[:], 0.0)
                    V.bn_aggr(fmv[:, 0, :], fst[:, 0, :])
                    nlink(c, V.bn_aggr(fmv[:, 1, :], fst[:, 1, :]), n=2)
                    V.tensor_scalar(fmv[:, :, 1], fmv[:, :, 1], 1e-5, None, ALU.add).then_inc(f_var, 1)
                if p == -3:
                    dve.wait_ge(f_rstd, k + 1)
                    nlink(c, V.scalar_tensor_tensor(frs[:, :, 1], fmv[:, :, 0], -1.0, frs[:, :, 0], ALU.mult,
                                                    ALU.mult), n=3)
                    for tt in range(TT):
                        last = V.tensor_scalar(xt[c.par][:, tt, :], xt[c.par][:, tt, :], frs[:, tt, 0:1],
                                               frs[:, tt, 1:2], ALU.mult, ALU.add)
                    last.then_inc(f_xn, 1)
                if 5 <= p < 5 + DB:
                    i, step = divmod(p - 5, 2)
                    blocks = (2 * i, 2 * i + 1)

                    def tap(m, q):
                        return V.scalar_tensor_tensor(ub[:, m, :], upre[:, m, q:q + T], cw[:, m, q:q + 1],
                                                      ub[:, m, :], ALU.mult, ALU.add)

                    if step == 0:
                        dve.wait_ge(f_used[i % 2], USES * k + 2 + i // 2)
                        if c.first() and i == 0:
                            dve.wait_ge(w_loaded[0], w_all[0])
                        flink(c, tap(blocks[0], 0), wait=False)
                        flink(c, tap(blocks[1], 0), wait=False)
                        flink.all_but(c, 1)
                        flink(c, tap(blocks[0], 1), wait=False)
                    else:
                        flink.all_but(c, 1)
                        flink(c, tap(blocks[1], 1), wait=False)
                        flink.all_but(c, 1)
                        tap(blocks[0], 2).then_inc(f_tap, 1)
                        flink.all_but(c, 0)
                        tap(blocks[1], 2).then_inc(f_tap, 1)
                        if i >= 2 or c.later(1):
                            dve.wait_ge(f_u, PAIRS * k + i - 1)
                        for j, m in enumerate(blocks):
                            dve.wait_ge(f_tap, DB * k + m + 1)
                            V.tensor_copy(upre[:, m, 0:K - 1], upre[:, m, T:T + K - 1])
                            ins = V.tensor_scalar(se[i % 2][:, j, :], ub[:, m, :], LEAST, None, ALU.max)
                        ins.then_inc(f_conv, 1)
                if p == 17:
                    dve.wait_ge(f_full[0], USES * k + 5)
                    V.tensor_copy(ssm[:], fp[0][:, 0:TT * XP].rearrange("p (a b) -> p a b", a=TT)).then_inc(f_used[0], 1)
                    dve.wait_ge(f_used[0], USES * k + 5)
                    flink(c, V.tensor_tensor(ssq[:], ssm[:], ssm[:], ALU.mult))
                    V.reduce_sum(ms[:, :, 0], ssq[:, :, 0:R], AX)
                    flink(c, V.reduce_sum(ms[:, :, 1:3], ssq[:, :, R:].rearrange("p a (g b) -> p a g b", g=2), AX))
                    V.tensor_scalar(ms[:, :, 0], ms[:, :, 0], 1.0 / R, 1e-6, ALU.mult, ALU.add)
                    V.tensor_scalar(ms[:, :, 1:3], ms[:, :, 1:3], 1.0 / NS, 1e-6, ALU.mult, ALU.add).then_inc(f_ms, 1)
                if p == 20:
                    dve.wait_ge(f_mrstd, k + 1)
                    if c.later(1):
                        dve.wait_ge(f_full[1], USES * (k - 1) + 6)
                    if c.later(2):
                        dve.wait_ge(y_added, BANKS * (k - 1))
                    for tt in range(TT):
                        V.tensor_scalar(dtn[:, tt, :], ssm[:, tt, 0:R], mr[:, tt, 0:1], None, ALU.mult)
                        V.scalar_tensor_tensor(bn[:, tt, :], ssm[:, tt, R:R + NS], mr[:, tt, 1:2], bw[:],
                                               ALU.mult, ALU.mult)
                        last = V.scalar_tensor_tensor(cn[c.par][:, tt, :], ssm[:, tt, R + NS:], mr[:, tt, 2:3],
                                                      cwt[:], ALU.mult, ALU.mult)
                    last.then_inc(f_bc, 1)
                    flink.close(c)
                if c.first():
                    scan_inputs(V, dve, dlink, c, p)

            def add_states(k, par, n, h):
                item = ITEMS * k + 2 * n + h
                for tt in range(TT):
                    dve.wait_ge(st_turned, 2 * item + tt + 1)
                    if n:
                        dve.wait_ge(y_added, 2 * item + tt - 3)
                    else:
                        dve.wait_ge(f_used[tt], USES * k + 4 + (0 if h == 0 else 2 - tt))
                        dve.wait_ge(f_bc, k + 1)
                    o = acc[par][:, tt, h * 512:(h + 1) * 512]
                    V.scalar_tensor_tensor(o, stt[TT * h + tt][:, :], cn[par][:, tt, n:n + 1], o, ALU.mult,
                                           ALU.add).then_inc(y_added, 1)

            def scan(c, p):
                n, h = divmod(p, 2)
                item = ITEMS * c.k + p
                dve.wait_ge(drive_ready, item + 1)
                dve.wait_ge(decay_ready, item + 1)
                w = st[p % RING][:].rearrange("p a t -> p (a t)")
                V.tensor_tensor_scan(w, decay[h][:].rearrange("p a t -> p (a t)"), w, 0.0, ALU.mult,
                                     ALU.add).then_inc(scan_done, 1)
                if p >= ADD_LAG:
                    add_states(c.k, c.par, *divmod(p - ADD_LAG, 2))
                elif c.later(1):
                    add_states(c.k - 1, 1 - c.par, *divmod(p - ADD_LAG + ITEMS, 2))

            def back(c, p):
                k = c.k
                if 7 <= p < 7 + PAIRS:
                    i = p - 7
                    dve.wait_ge(r_full[i % 2], before(c, Y + i // 2) + 1)
                    dve.wait_ge(gated[i // 2], 2 * k + i % 2 + 1)
                    s = slice(2 * i, 2 * i + 2)
                    V.tensor_tensor(y[:, s, :], two(bp[i % 2]), y[:, s, :], ALU.mult).then_inc(r_used[i % 2], 1)
                if p in (15, 19):
                    tt = (p - 15) // 4
                    if tt == 0:
                        dve.wait_ge(xr_in, 16 * k + 16)
                    dve.wait_ge(r_full[tt], before(c, ATTN) + 1)
                    V.tensor_tensor(xr[:, tt, :], bp[tt][:, :], xr[:, tt, :], ALU.add).then_inc(r_used[tt], 1)
                    dve.wait_ge(r_used[tt], before(c, ATTN) + 1)
                    rlink(c, V.bn_stats(bst[:, tt, :], xr[:, tt, :]), tt == 1)
                    if tt:
                        V.memset(unused[:], 0.0)
                        for t2 in range(TT):
                            rlink(c, V.bn_aggr(bmv[:, t2, :], bst[:, t2, :]), t2 == TT - 1)
                        V.tensor_scalar(bmv[:, :, 1], bmv[:, :, 1], 1e-5, None, ALU.add).then_inc(r_var, 1)
                if p == 21:
                    dve.wait_ge(r_rstd, k + 1)
                    rlink(c, V.scalar_tensor_tensor(brs[:, :, 1], bmv[:, :, 0], -1.0, brs[:, :, 0], ALU.mult, ALU.mult))
                    for tt in range(TT):
                        last = V.tensor_scalar(x2[1 - c.par][:, tt, :], xr[:, tt, :], brs[:, tt, 0:1],
                                               brs[:, tt, 1:2], ALU.mult, ALU.add)
                    last.then_inc(r_xn, 1)
                if p in (32, 34):
                    tt = (p - 32) // 2
                    dve.wait_ge(r_full[tt], before(c, LIN) + 1)
                    V.tensor_tensor(xr[:, tt, :], bp[tt][:, :], xr[:, tt, :], ALU.add).then_inc(r_used[tt], 1)
                if p == ITEMS - 1:
                    rlink.close(c)

            def gates(c, p):
                if c.first() and p == 20:
                    dve.wait_ge(fa_pe, 2)
                if p in (21, 23, 29, 33):
                    i = (21, 23, 29, 33).index(p)
                    s = slice(2 * i, 2 * i + 2)
                    dve.wait_ge(r_used[i % 2], before_gates(c, i // 2) + 1)
                    if i >= 2:
                        dve.wait_ge(gated[0], 2 * c.k + i - 1)
                    elif c.later(1):
                        dve.wait_ge(gated[1], 2 * c.k + i - 1)
                    V.tensor_scalar(ge[i % 2][:], y[:, s, :], LEAST, None, ALU.max).then_inc(g_cut, 1)
                if p in (24, 32):
                    i = (24, 32).index(p)
                    s = slice(2 * i, 2 * i + 2)
                    dve.wait_ge(g_s, PAIRS * c.k + i + 1)
                    V.tensor_tensor(y[:, s, :], y[:, s, :], ge[i % 2][:], ALU.mult).then_inc(gated[0], 1)

            def scanned():
                for p in range(ITEMS - ADD_LAG, ITEMS):
                    add_states(NC - 1, 1, *divmod(p, 2))

            over_chunks(dve, front, scan, back, gates, setup, scanned)

            t = [0]

            def tl(ins):
                t[0] += 1
                ins.then_inc(t_link, 1)
                dve.wait_ge(t_link, t[0])

            def each(v):
                return v[:, :, None].broadcast_to([P, lt, E])

            dve.wait_ge(t_act, 2)
            tl(V.reduce_max(tmx[:, 0:1], tw[0][:].rearrange("p a b -> p (a b)"), AX))
            tl(V.reduce_max(tmx[:, 1:2], tw[1][:].rearrange("p a b -> p (a b)"), AX))
            dve.wait_ge(t_red, 1)
            tl(V.tensor_scalar(tmr[:], tmr[:], 1e-6, 2.0, ALU.max, ALU.mult))
            tl(V.reciprocal(tmr[:], tmr[:]))
            tl(V.tensor_scalar(tw[2][:], ds[:], tmr[:, 1:2], None, ALU.mult))
            tl(V.scalar_tensor_tensor(tw[2][:], hs[:], tmr[:, 0:1], tw[2][:], ALU.mult, ALU.add))
            tl(V.reduce_max(tm[:, 0, :], tw[2][:], AX))
            tl(V.tensor_tensor(tw[2][:], tw[2][:], each(tm[:, 0, :]), ALU.subtract))
            dve.wait_ge(t_act, 3)
            tl(V.reduce_sum(tm[:, 1, :], tw[2][:], AX))
            tl(V.reciprocal(tm[:, 1, :], tm[:, 1, :]))
            tl(V.tensor_tensor(tw[2][:], tw[2][:], each(tm[:, 1, :]), ALU.mult))
            for i in range(lt):
                last = V.max(tw[4][:, i, :], tw[2][:, i, :])
            tl(last)
            tl(V.tensor_tensor(tw[3][:], tw[2][:], each(tw[4][:, :, 1]), ALU.subtract))
            dve.wait_ge(t_act, 5)
            tl(V.reciprocal(tw[3][:], tw[3][:]))
            tl(V.tensor_tensor(tw[2][:], tw[2][:], tw[3][:], ALU.mult))
            tl(V.reduce_sum(tm[:, 2, :], tw[2][:], AX))
            tl(V.tensor_scalar(tm[:, 2, :], tm[:, 2, :], 1e-9, None, ALU.add))
            tl(V.reciprocal(tm[:, 2, :], tm[:, 2, :]))
            tl(V.tensor_tensor(tw[0][:], tw[2][:], each(tm[:, 2, :]), ALU.mult))
            assert t[0] == TAIL_W, t[0]
            dve.wait_ge(z_in, 16)
            pbanks = [bp[0], bp[1], stt[0], stt[1]]
            for q in range(4):
                dve.wait_ge(t_pe, 4 + q + 1)
                z = zall[:, q * 512:(q + 1) * 512].rearrange("p (a b) -> p a b", b=2)
                pm = pbanks[q][0:RANK, 0:256][:, :, None].broadcast_to([RANK, 256, 2])
                V.scalar_tensor_tensor(z, z, 0.5, pm, ALU.mult, ALU.mult).then_inc(t_link, 1)
            dve.wait_ge(base_in, 16 * len(base_tiles))
            banks = [fp[0], fp[1], stt[2], stt[3]]
            for i in range(lt):
                dve.wait_ge(t_pe, 8 + i + 1)
                o = base_tiles[i // 4][:, i % 4, :]
                V.tensor_tensor(o, banks[i % 4][:, :], o, ALU.add).then_inc(out_ready, 1)



INS = ["x", "w_in", "conv_w", "conv_b", "w_x", "dt_w", "b_w", "c_w", "w_dt", "dt_bias", "a_neg", "d_par", "w_out",
       "ffn_w", "ffn_b", "ffn_a", "bmat", "limes", "limes_t", "cond", "wmod"]


def kernel(**inputs):
    import numpy as np
    import concourse.bacc as bacc
    from concourse.bass_utils import run_bass_kernel_spmd as run

    v = {k: np.asarray(a) for k, a in inputs.items()}

    def tiles(a):
        return a.reshape(a.shape[0] // P, P, -1).transpose(1, 0, 2)

    def column(a):
        return a.reshape(-1, P).T

    at = "L0_attn_"
    data = {
        "x": v[at + "hidden_states"],
        "w_in": tiles(v[at + "W_in"].T),
        "conv_w": tiles(v[at + "conv_w"]),
        "conv_b": column(v[at + "conv_b"]),
        "w_x": tiles(v[at + "Wx"].T),
        "dt_w": v[at + "dt_ln_w"][:, None],
        "b_w": v[at + "b_ln_w"],
        "c_w": v[at + "c_ln_w"],
        "w_dt": v[at + "Wdt"].T,
        "dt_bias": column(v[at + "dt_bias"]),
        "a_neg": tiles(v[at + "A"]).transpose(0, 2, 1),
        "d_par": column(v[at + "D_param"]),
        "w_out": tiles(v[at + "W_out"].T),
        "ffn_w": tiles(v["L0_ffn_W"].T),
        "ffn_b": v["L0_ffn_b"][None, :],
        "ffn_a": tiles(v["L0_ffn_A"]),
        "bmat": v["L0_ffn_Bmat"],
        "limes": v["L0_ffn_LiMEs"],
        "limes_t": v["L0_ffn_LiMEs"].T,
        "cond": column(v["L0_c"][0]),
        "wmod": v["L0_wmod"],
    }
    nc = bacc.Bacc("TRN2", target_bir_lowering=False, num_devices=1)
    arrays, args = {}, []
    for name in INS:
        a = np.ascontiguousarray(data[name])
        arrays[name] = a
        args.append(nc.dram_tensor(name, a.shape, mybir.dt.from_np(a.dtype), kind="ExternalInput").ap())
    out = nc.dram_tensor("out", (1, L, H), mybir.dt.float32, kind="ExternalOutput").ap()
    build(nc, *args, out)
    r = run(nc, [arrays], core_ids=[0])
    return r.results[0]["out"]
```
